# Optimizing a Trainium2 kernel written in Bass

```python
import numpy as np
import jax
import jax.numpy as jnp

def _softmax(x, axis=-1):
    return jax.nn.softmax(x, axis=axis)

def _gelu(x):
    return jax.nn.gelu(x, approximate=True)

def _silu(x):
    return jax.nn.silu(x)

def _sigmoid(x):
    return jax.nn.sigmoid(x)

def _layernorm(x, axis=-1, eps=1e-05):
    m = jnp.mean(x, axis=axis, keepdims=True)
    v = jnp.var(x, axis=axis, keepdims=True)
    return (x - m) / jnp.sqrt(v + eps)

def _scatter_add(tgt, idx, src, axis=0):
    return tgt.at[idx].add(src)

def _segment_sum(src, seg, n):
    return jax.ops.segment_sum(src, seg, n)
kernel_name = 'mk_decoder_preln_d2_seqx_r8_8bdcdc'

def setup_inputs(seed: int=0):
    np.random.seed(seed)
    _w = jnp.asarray

    def _rec_inputs():
        import jax
        import jax.numpy as jnp
        _rk = jax.random.key(seed)
        x = -0.000125 + 0.9999 * jax.random.normal(jax.random.fold_in(_rk, 1), (16, 64, 256), jnp.float32)
        _lenS = 64 - jax.random.randint(jax.random.fold_in(_rk, 7), (16,), 0, max(1, 64 // 4) + 1, jnp.int32)
        _lenS2 = 64 - jax.random.randint(jax.random.fold_in(_rk, 8), (16,), 0, max(1, 64 // 4) + 1, jnp.int32)
        _ctx_2048P = jax.random.normal(jax.random.fold_in(_rk, 11), (16, 16, 256), jnp.float32)
        _ctx_2048c = jax.random.dirichlet(jax.random.fold_in(_rk, 511), 0.3 * jnp.ones((16,), jnp.float32), (16, 64))
        _ctx_2048t = jnp.einsum('bsk,bkd->bsd', _ctx_2048c, _ctx_2048P)
        _ctx_2048t = _ctx_2048t * jax.lax.rsqrt(jnp.mean(jnp.square(_ctx_2048t)) + 1e-12) * 0.953939
        ctx_2048 = -0.000514642 + 1.00011 * (_ctx_2048t + 0.3 * jax.random.normal(jax.random.fold_in(_rk, 611), (16, 64, 256), jnp.float32))
        _validS = jnp.arange(64)[None, :] < _lenS[:, None]
        _validS2 = jnp.arange(64)[None, :] < _lenS2[:, None]
        _causal = jnp.tril(jnp.ones((64, 64), dtype=bool))
        mask_BxS2_bk0 = jnp.logical_not(jnp.broadcast_to(_validS2[:, :], (16, 64)))
        return (x, ctx_2048, mask_BxS2_bk0)
    x, ctx_2048, mask_BxS2_bk0 = _rec_inputs()

    def _L0_attn_setup():
        import math
        import jax, jax.numpy as jnp
        import numpy as np
        D_MODEL = 256
        NUM_HEADS = 16
        D_HEAD = D_MODEL // NUM_HEADS
        THETA = 10000.0

        def _rope_tables(seq_len, d_head):
            idx = jnp.arange(0, d_head, 2, dtype=jnp.float32)
            inv_freq = THETA ** (-idx / d_head)
            angles = jnp.arange(seq_len, dtype=jnp.float32)[:, None] * inv_freq[None, :]
            return (jnp.cos(angles), jnp.sin(angles))

        def _apply_rope(x, cos, sin):
            B, H, S, d = x.shape
            xp = x.reshape(B, H, S, d // 2, 2)
            xe, xo = (xp[..., 0], xp[..., 1])
            rot = jnp.stack([xe * cos - xo * sin, xe * sin + xo * cos], axis=-1)
            return rot.reshape(B, H, S, d)
        key = jax.random.key(seed)
        k_x, k_q, k_k, k_v, k_o = jax.random.split(key, 5)
        std = math.sqrt(2.0 / (D_MODEL + D_MODEL))
        x = jax.random.normal(k_x, (4, 256, D_MODEL), dtype=jnp.float32)
        Wq = jax.random.normal(k_q, (D_MODEL, D_MODEL), dtype=jnp.float32) * std
        Wk = jax.random.normal(k_k, (D_MODEL, D_MODEL), dtype=jnp.float32) * std
        Wv = jax.random.normal(k_v, (D_MODEL, D_MODEL), dtype=jnp.float32) * std
        Wo = jax.random.normal(k_o, (D_MODEL, D_MODEL), dtype=jnp.float32) * std
        return {'x': x, 'Wq': Wq, 'Wk': Wk, 'Wv': Wv, 'Wo': Wo}
    _L0_attn_all = _L0_attn_setup()
    _L0_attn_in = {k: v for k, v in _L0_attn_all.items() if k in ('Wq', 'Wk', 'Wv', 'Wo')}
    del _L0_attn_all

    def _L0_xattn_setup():
        import jax, jax.numpy as jnp
        import numpy as np
        key = jax.random.key(seed)
        k1, k2, k3 = jax.random.split(key, 3)
        B, S, D, M = (8, 256, 256, 128)
        hidden_states = jax.random.normal(k1, (B, S, D), dtype=jnp.float32)
        memory_tokens = jax.random.normal(k2, (B, M, D), dtype=jnp.float32)
        memory_mask = jax.random.randint(k3, (B, M), 0, 2).astype(jnp.bool_)
        return {'hidden_states': hidden_states, 'memory_tokens': memory_tokens, 'memory_mask': memory_mask}
    _L0_xattn_all = _L0_xattn_setup()
    _L0_xattn_in = {k: v for k, v in _L0_xattn_all.items() if k in ()}
    del _L0_xattn_all

    def _L0_ffn_setup():
        import jax, jax.numpy as jnp
        import numpy as np
        E, TOPK, H, I, NSH = (8, 2, 256, 640, 2)
        B, S = (2, 128)
        key = jax.random.key(seed)
        ks = jax.random.split(key, 8)
        sc = 0.02
        return {'x': jax.random.normal(ks[0], (B, S, H), dtype=jnp.float32), 'w_router': jax.random.normal(ks[1], (E, H), dtype=jnp.float32), 'wg': jax.random.normal(ks[2], (E, I, H), dtype=jnp.float32) * sc, 'wu': jax.random.normal(ks[3], (E, I, H), dtype=jnp.float32) * sc, 'wd': jax.random.normal(ks[4], (E, H, I), dtype=jnp.float32) * sc, 'sg': jax.random.normal(ks[5], (NSH, I, H), dtype=jnp.float32) * sc, 'su': jax.random.normal(ks[6], (NSH, I, H), dtype=jnp.float32) * sc, 'sd': jax.random.normal(ks[7], (NSH, H, I), dtype=jnp.float32) * sc}
    _L0_ffn_all = _L0_ffn_setup()
    _L0_ffn_in = {k: v for k, v in _L0_ffn_all.items() if k in ('w_router', 'wg', 'wu', 'wd', 'sg', 'su', 'sd')}
    del _L0_ffn_all

    def _L1_attn_setup():
        import jax, jax.numpy as jnp
        import numpy as np
        import math
        D_MODEL = 256
        N_HEADS = 16
        N_KV = 4
        HEAD_DIM = D_MODEL // N_HEADS
        SUB = HEAD_DIM // 2
        WINDOW = 64
        THETA = 10000.0
        B, S = (1, 256)

        def rotate_half(x):
            x1, x2 = (x[..., :x.shape[-1] // 2], x[..., x.shape[-1] // 2:])
            return jnp.concatenate([-x2, x1], axis=-1)
        key = jax.random.key(seed)
        ks = jax.random.split(key, 6)
        std = 0.02
        x = jax.random.normal(ks[0], (B, S, D_MODEL), dtype=jnp.float32)
        Wq = jax.random.normal(ks[1], (D_MODEL, N_HEADS * HEAD_DIM), dtype=jnp.float32) * std
        Wk = jax.random.normal(ks[2], (D_MODEL, N_KV * HEAD_DIM), dtype=jnp.float32) * std
        Wv = jax.random.normal(ks[3], (D_MODEL, N_KV * HEAD_DIM), dtype=jnp.float32) * std
        Wo = jax.random.normal(ks[4], (N_HEADS * HEAD_DIM, D_MODEL), dtype=jnp.float32) * std
        lam = jnp.full((N_HEADS,), 0.1, dtype=jnp.float32)
        return {'x': x, 'Wq': Wq, 'Wk': Wk, 'Wv': Wv, 'Wo': Wo, 'lam': lam}
    _L1_attn_all = _L1_attn_setup()
    _L1_attn_in = {k: v for k, v in _L1_attn_all.items() if k in ('Wq', 'Wk', 'Wv', 'Wo', 'lam')}
    del _L1_attn_all

    def _L1_xattn_setup():
        import jax, jax.numpy as jnp
        import numpy as np
        N_HEAD = 8
        key = jax.random.key(seed)
        k1, k2, k3 = jax.random.split(key, 3)
        b, d, m = (4, 128, 256)
        c, n = (128, 256)
        q = jax.random.normal(k1, (b, d, m), dtype=jnp.float32)
        k = jax.random.normal(k2, (d // d * b, d, n), dtype=jnp.float32).reshape(b, d, n)
        v = jax.random.normal(k3, (b, c, n), dtype=jnp.float32)
        return {'q': q, 'k': k, 'v': v}
    _L1_xattn_all = _L1_xattn_setup()
    _L1_xattn_in = {k: v for k, v in _L1_xattn_all.items() if k in ()}
    del _L1_xattn_all

    def _L1_ffn_setup():
        import jax, jax.numpy as jnp
        import numpy as np
        TOP_K = 4
        NUM_EXPERTS = 16
        key = jax.random.key(seed)
        ks = jax.random.split(key, 6)
        B, S, H, I, E = (2, 128, 256, 224, NUM_EXPERTS)
        return {'x': jax.random.normal(ks[0], (B, S, H), dtype=jnp.float32), 'router_w': jax.random.normal(ks[1], (E, H), dtype=jnp.float32) * 0.02, 'expert_bias': jnp.zeros((E,), dtype=jnp.float32), 'gate_proj': jax.random.normal(ks[2], (E, H, I), dtype=jnp.float32) * 0.02, 'up_proj': jax.random.normal(ks[3], (E, H, I), dtype=jnp.float32) * 0.02, 'down_proj': jax.random.normal(ks[4], (E, I, H), dtype=jnp.float32) * 0.02}
    _L1_ffn_all = _L1_ffn_setup()
    _L1_ffn_in = {k: v for k, v in _L1_ffn_all.items() if k in ('router_w', 'expert_bias', 'gate_proj', 'up_proj', 'down_proj')}
    del _L1_ffn_all
    return {'x': x, 'ctx_2048': ctx_2048, 'mask_BxS2_bk0': mask_BxS2_bk0, 'L0_attn_Wq': _L0_attn_in['Wq'], 'L0_attn_Wk': _L0_attn_in['Wk'], 'L0_attn_Wv': _L0_attn_in['Wv'], 'L0_attn_Wo': _L0_attn_in['Wo'], 'L0_ffn_w_router': _L0_ffn_in['w_router'], 'L0_ffn_wg': _L0_ffn_in['wg'], 'L0_ffn_wu': _L0_ffn_in['wu'], 'L0_ffn_wd': _L0_ffn_in['wd'], 'L0_ffn_sg': _L0_ffn_in['sg'], 'L0_ffn_su': _L0_ffn_in['su'], 'L0_ffn_sd': _L0_ffn_in['sd'], 'L1_attn_Wq': _L1_attn_in['Wq'], 'L1_attn_Wk': _L1_attn_in['Wk'], 'L1_attn_Wv': _L1_attn_in['Wv'], 'L1_attn_Wo': _L1_attn_in['Wo'], 'L1_attn_lam': _L1_attn_in['lam'], 'L1_ffn_router_w': _L1_ffn_in['router_w'], 'L1_ffn_expert_bias': _L1_ffn_in['expert_bias'], 'L1_ffn_gate_proj': _L1_ffn_in['gate_proj'], 'L1_ffn_up_proj': _L1_ffn_in['up_proj'], 'L1_ffn_down_proj': _L1_ffn_in['down_proj']}

def reference(x, ctx_2048, mask_BxS2_bk0, L0_attn_Wq, L0_attn_Wk, L0_attn_Wv, L0_attn_Wo, L0_ffn_w_router, L0_ffn_wg, L0_ffn_wu, L0_ffn_wd, L0_ffn_sg, L0_ffn_su, L0_ffn_sd, L1_attn_Wq, L1_attn_Wk, L1_attn_Wv, L1_attn_Wo, L1_attn_lam, L1_ffn_router_w, L1_ffn_expert_bias, L1_ffn_gate_proj, L1_ffn_up_proj, L1_ffn_down_proj):
    import jax
    import jax.numpy as jnp

    def _L0_attn_ref(x, Wq, Wk, Wv, Wo):
        import math
        import jax, jax.numpy as jnp
        import numpy as np
        D_MODEL = 256
        NUM_HEADS = 16
        D_HEAD = D_MODEL // NUM_HEADS
        THETA = 10000.0

        def _rope_tables(seq_len, d_head):
            idx = jnp.arange(0, d_head, 2, dtype=jnp.float32)
            inv_freq = THETA ** (-idx / d_head)
            angles = jnp.arange(seq_len, dtype=jnp.float32)[:, None] * inv_freq[None, :]
            return (jnp.cos(angles), jnp.sin(angles))

        def _apply_rope(x, cos, sin):
            B, H, S, d = x.shape
            xp = x.reshape(B, H, S, d // 2, 2)
            xe, xo = (xp[..., 0], xp[..., 1])
            rot = jnp.stack([xe * cos - xo * sin, xe * sin + xo * cos], axis=-1)
            return rot.reshape(B, H, S, d)
        B, S, D = x.shape
        H, dh = (NUM_HEADS, D_HEAD)

        def proj(W):
            y = jnp.einsum('bsi,oi->bso', x, W)
            return y.reshape(B, S, H, dh).transpose(0, 2, 1, 3)
        q, k, v = (proj(Wq), proj(Wk), proj(Wv))
        cos, sin = _rope_tables(S, dh)
        q = _apply_rope(q, cos, sin)
        k = _apply_rope(k, cos, sin)
        scores = jnp.einsum('bhqd,bhkd->bhqk', q.astype(jnp.float32), k.astype(jnp.float32)) / math.sqrt(dh)
        causal = jnp.tril(jnp.ones((S, S), dtype=bool))
        scores = jnp.where(causal, scores, jnp.finfo(jnp.float32).min)
        probs = jax.nn.softmax(scores, axis=-1).astype(v.dtype)
        attn = jnp.einsum('bhqk,bhkd->bhqd', probs, v)
        attn = attn.transpose(0, 2, 1, 3).reshape(B, S, D)
        return jnp.einsum('bsi,oi->bso', attn, Wo)

    def _L0_xattn_ref(hidden_states, memory_tokens, memory_mask):
        import jax, jax.numpy as jnp
        import numpy as np
        B, S, D = hidden_states.shape
        scale = 1.0 / jnp.sqrt(jnp.asarray(D, hidden_states.dtype))
        scores = jnp.einsum('bsd,bmd->bsm', hidden_states, memory_tokens) * scale
        neg_inf = jnp.asarray(-1e+30, scores.dtype)
        scores = jnp.where(memory_mask[:, None, :], scores, neg_inf)
        attn = jax.nn.softmax(scores, axis=-1)
        readout = jnp.einsum('bsm,bmd->bsd', attn, memory_tokens)
        valid_b = jnp.any(memory_mask, axis=-1)
        out = jnp.where(valid_b[:, None, None], readout, jnp.zeros_like(readout))
        return out

    def _L0_ffn_ref(x, w_router, wg, wu, wd, sg, su, sd):
        import jax, jax.numpy as jnp
        import numpy as np
        E, TOPK, H, I, NSH = (8, 2, 256, 640, 2)
        B, S = (2, 128)
        b, s, h = x.shape
        xt = x.reshape(-1, h)
        T = xt.shape[0]
        logits = jnp.einsum('th,eh->te', xt.astype(jnp.float32), w_router.astype(jnp.float32))
        scores = jax.nn.sigmoid(logits)
        topk_w, topk_i = jax.lax.top_k(scores, TOPK)
        topk_w = topk_w / jnp.sum(topk_w, axis=-1, keepdims=True)
        comb = jnp.zeros((T, E), dtype=xt.dtype)
        comb = comb.at[jnp.arange(T)[:, None], topk_i].add(topk_w.astype(xt.dtype))
        gate = jax.nn.silu(jnp.einsum('th,eih->tei', xt, wg))
        up = jnp.einsum('th,eih->tei', xt, wu)
        expert_out = jnp.einsum('tei,ehi->teh', gate * up, wd)
        out = jnp.einsum('te,teh->th', comb, expert_out)
        sgate = jax.nn.silu(jnp.einsum('th,jih->tji', xt, sg))
        sup = jnp.einsum('th,jih->tji', xt, su)
        out = out + jnp.einsum('tji,jhi->th', sgate * sup, sd)
        return out.reshape(b, s, h)

    def _L1_attn_ref(x, Wq, Wk, Wv, Wo, lam):
        import jax, jax.numpy as jnp
        import numpy as np
        import math
        D_MODEL = 256
        N_HEADS = 16
        N_KV = 4
        HEAD_DIM = D_MODEL // N_HEADS
        SUB = HEAD_DIM // 2
        WINDOW = 64
        THETA = 10000.0
        B, S = (1, 256)

        def rotate_half(x):
            x1, x2 = (x[..., :x.shape[-1] // 2], x[..., x.shape[-1] // 2:])
            return jnp.concatenate([-x2, x1], axis=-1)
        b, s, _ = x.shape
        q = (x @ Wq).reshape(b, s, N_HEADS, HEAD_DIM).transpose(0, 2, 1, 3)
        k = (x @ Wk).reshape(b, s, N_KV, HEAD_DIM).transpose(0, 2, 1, 3)
        v = (x @ Wv).reshape(b, s, N_KV, HEAD_DIM).transpose(0, 2, 1, 3)
        inv_freq = 1.0 / THETA ** (jnp.arange(0, HEAD_DIM, 2, dtype=jnp.float32) / HEAD_DIM)
        t = jnp.arange(s, dtype=jnp.float32)
        freqs = t[:, None] * inv_freq[None, :]
        emb = jnp.concatenate([freqs, freqs], axis=-1)
        cos, sin = (jnp.cos(emb), jnp.sin(emb))
        q = q * cos + rotate_half(q) * sin
        k = k * cos + rotate_half(k) * sin
        n_rep = N_HEADS // N_KV
        k = jnp.repeat(k, n_rep, axis=1)
        v = jnp.repeat(v, n_rep, axis=1)
        scale = 1.0 / math.sqrt(SUB)
        q1, q2 = (q[..., :SUB], q[..., SUB:])
        k1, k2 = (k[..., :SUB], k[..., SUB:])
        a1 = jnp.einsum('bhqd,bhkd->bhqk', q1, k1) * scale
        a2 = jnp.einsum('bhqd,bhkd->bhqk', q2, k2) * scale
        row = jnp.arange(s)[:, None]
        col = jnp.arange(s)[None, :]
        allowed = (col <= row) & (col >= row - WINDOW + 1)
        neg = jnp.where(allowed, 0.0, -jnp.inf).astype(a1.dtype)
        a1 = a1 + neg
        a2 = a2 + neg
        p1 = jax.nn.softmax(a1.astype(jnp.float32), axis=-1).astype(x.dtype)
        p2 = jax.nn.softmax(a2.astype(jnp.float32), axis=-1).astype(x.dtype)
        diff = jax.nn.relu(p1 - lam[None, :, None, None] * p2)
        diff = diff / (diff.sum(axis=-1, keepdims=True) + 1e-06)
        out = jnp.einsum('bhqk,bhkd->bhqd', diff, v)
        out = out.transpose(0, 2, 1, 3).reshape(b, s, N_HEADS * HEAD_DIM)
        return out @ Wo

    def _L1_xattn_ref(q, k, v):
        import jax, jax.numpy as jnp
        import numpy as np
        N_HEAD = 8
        b, d, m = q.shape
        c = v.shape[1]
        h = N_HEAD
        qh = q.reshape(b * h, d // h, m)
        kh = k.reshape(b * h, d // h, -1)
        vh = v.reshape(b * h, c // h, -1)
        scale = 1.0 / jnp.sqrt(jnp.asarray(d // h, dtype=q.dtype))
        qk = jnp.einsum('bdm,bdn->bmn', qh, kh) * scale
        sm = jax.nn.softmax(qk, axis=-1)
        ret = jnp.einsum('bmn,bcn->bcm', sm, vh)
        return ret.reshape(b, c, m)

    def _L1_ffn_ref(x, router_w, expert_bias, gate_proj, up_proj, down_proj):
        import jax, jax.numpy as jnp
        import numpy as np
        TOP_K = 4
        NUM_EXPERTS = 16
        logits = jnp.einsum('bsh,eh->bse', x, router_w) + expert_bias
        scores = jax.nn.softmax(logits, axis=-1)
        top_w, top_idx = jax.lax.top_k(scores, TOP_K)
        top_w = top_w / jnp.sum(top_w, axis=-1, keepdims=True)
        g = jnp.einsum('bsh,khe->bske', x, gate_proj)
        u = jnp.einsum('bsh,khe->bske', x, up_proj)
        act = jax.nn.silu(g) * u
        out = jnp.einsum('bske,keh->bskh', act, down_proj)
        sel = jnp.take_along_axis(out, top_idx[..., None], axis=2)
        return jnp.sum(sel * top_w[..., None], axis=2)
    x = x + _L0_attn_ref(_layernorm(x, axis=-1), L0_attn_Wq, L0_attn_Wk, L0_attn_Wv, L0_attn_Wo)
    x = x + _L0_xattn_ref(_layernorm(x, axis=-1), ctx_2048, mask_BxS2_bk0)
    x = x + _L0_ffn_ref(_layernorm(x, axis=-1), L0_ffn_w_router, L0_ffn_wg, L0_ffn_wu, L0_ffn_wd, L0_ffn_sg, L0_ffn_su, L0_ffn_sd)
    x = x + _L1_attn_ref(_layernorm(x, axis=-1), L1_attn_Wq, L1_attn_Wk, L1_attn_Wv, L1_attn_Wo, L1_attn_lam)
    x = x + _L1_xattn_ref(_layernorm(x, axis=-1), ctx_2048, ctx_2048)
    x = x + _L1_ffn_ref(_layernorm(x, axis=-1), L1_ffn_router_w, L1_ffn_expert_bias, L1_ffn_gate_proj, L1_ffn_up_proj, L1_ffn_down_proj)
    return x

_drawn_inputs = setup_inputs


def setup_inputs(seed=0):
    import zlib

    import numpy as np

    out = dict(_drawn_inputs(seed))
    spreads = {'L1_attn_lam': (0.10000000149011612, 0.6), 'L1_ffn_expert_bias': (0.0, 0.8)}
    factors = {'L0_ffn_w_router': 4.809,
     'L0_ffn_wg': 4.149,
     'L0_ffn_wu': 4.128,
     'L0_ffn_wd': 4.104,
     'L1_attn_Wq': 8.0,
     'L1_attn_Wk': 8.0,
     'L1_ffn_router_w': 8.0,
     'L1_ffn_gate_proj': 8.0,
     'L1_ffn_up_proj': 8.0,
     'L1_ffn_down_proj': 8.0}
    for name, (base, spread) in spreads.items():
        noise = np.random.default_rng([zlib.crc32(name.encode()), seed]).standard_normal(out[name].shape)
        drawn = base * np.exp(spread * noise) if base else spread * noise
        out[name] = jnp.asarray(drawn.astype(out[name].dtype))
    for name, factor in factors.items():
        out[name] = (out[name] * factor).astype(out[name].dtype)
    return out
```

```python
from contextlib import ExitStack

import numpy as np

import concourse.bass as bass
from concourse import mybir

F32 = mybir.dt.float32
F32R = mybir.dt.float32r
BF16 = mybir.dt.bfloat16
U8 = mybir.dt.uint8
ALU = mybir.AluOpType
ACT = mybir.ActivationFunctionType
AX = mybir.AxisListType.X

P = 128
BATCH, SEQ, D = 16, 64, 256
TOKENS = BATCH * SEQ
TILES = TOKENS // P
C = D // P
B2 = P // SEQ
HEADS, HD = 16, 16
PAIRS = HEADS // 2
CH = HEADS // C
KV = 4
JP = 2
EPS = 1e-5
NEG = -1e30
XH = 8
GT = P // 8
SB, G4 = 4, 4

E0, SHARED0, I0, TOP0 = 8, 2, 640, 2
E1, I1, TOP1 = 16, 224, 4
CHUNKS0 = (E0 + SHARED0) * I0 // P
CHUNKS1 = E1 * I1 // P
HALVES, HT = 2, TOKENS // 2

K_ID, K_COS, K_SIN0, K_SIN1, K_H16, K_B8, K_CAUSAL, K_TRI0, K_TRI1, K_ONE4, K_COS1 = (
    0, 128, 144, 160, 176, 184, 192, 256, 320, 576, 580)
K_ALL = 596
A_QK, A_V, A_O, A_R = 0, 512, 768, 1024
A_ALL = 1032
W_QK, W_V, W_O, W_R = 0, 320, 384, 640
W_ALL = 656


def end_program(nc, semaphores):
    nc.clear_and_free_semaphores(semaphores)
    nc.all_engine_barrier()


class Steps:

    def __init__(self, eng, sem, per_round):
        self.eng, self.sem, self.per_round = eng, sem, per_round

    def start(self, i):
        self.base, self.n = i * self.per_round, 0

    def done(self, ins):
        ins.then_inc(self.sem, 1)
        self.n += 1

    def wait(self):
        self.eng.wait_ge(self.sem, self.base + self.n)

    def end(self):
        assert self.n == self.per_round, (self.n, self.per_round)


def bc(ap, axis, n):
    ap = ap.unsqueeze(axis)
    shape = list(ap.shape)
    shape[axis] = n
    return ap.broadcast_to(shape)


def decoder_kernel(nc, x, consts, w_attn0, ctx_rows, ctx_cols, ctx_lhs, mask, w_ffn0, w_attn1, lam, bias1, w_ffn1,
                   out, ctx_dram, comb0_dram, comb1_dram):
    with ExitStack() as whole:
        X = whole.enter_context(nc.sbuf_tensor("X", [P, TILES, D], F32))
        xh = whole.enter_context(nc.sbuf_tensor("xh", [P, C, TOKENS], F32R))
        xl = whole.enter_context(nc.sbuf_tensor("xl", [P, C, TOKENS], F32R))
        K = whole.enter_context(nc.sbuf_tensor("K", [P, K_ALL], F32))
        ps = whole.enter_context(nc.psum_tensor("ps", [P, 8, 512], F32))
        attention0(nc, x, consts, w_attn0, ctx_rows, ctx_cols, mask, X, xh, xl, K, ps, comb0_dram)
        experts(nc, "f0", w_ffn0, comb0_dram, CHUNKS0, 10, I0, 5, 4, X, xh, xl, K, ps, None)
        attention1(nc, w_attn1, ctx_rows, ctx_lhs, lam, bias1, X, xh, xl, K, ps, ctx_dram, comb1_dram)
        experts(nc, "f1", w_ffn1, comb1_dram, CHUNKS1, 7, I1, 7, 7, X, xh, xl, K, ps, out)


def rank_and_combine(nc, dve, step, scores, tri, n_experts, top, cmp, eq, rank, sums, comb):
    E = n_experts
    other = bc(scores[:, :, :], 2, E)
    own = bc(scores[:, :, :], 3, E)
    c4 = cmp[:, :].rearrange("p (t e f) -> p t e f", t=TILES, e=E)
    q4 = eq[:, :].rearrange("p (t e f) -> p t e f", t=TILES, e=E)
    nc.vector.tensor_tensor(c4, other, own, ALU.is_gt)
    step.done(nc.vector.tensor_tensor(q4, other, own, ALU.is_equal))
    step.wait()
    q3 = eq[:, :].rearrange("p (t f) -> p t f", t=TILES)
    step.done(nc.vector.tensor_tensor(q3, q3, bc(tri, 1, TILES), ALU.mult))
    step.wait()
    step.done(nc.vector.tensor_tensor(cmp[:, :], cmp[:, :], eq[:, :], ALU.add))
    step.wait()
    step.done(nc.vector.tensor_reduce(rank[:, :], cmp[:, :].rearrange("p (t f) -> p t f", f=E), AX, ALU.add))
    step.wait()
    step.done(nc.vector.tensor_scalar(rank[:, :], rank[:, :], float(top) - 0.5, None, ALU.is_lt))
    step.wait()
    r3 = rank[:, :].rearrange("p (t e) -> p t e", t=TILES)
    step.done(nc.vector.tensor_tensor(comb[:, :, :], scores[:, :, :], r3, ALU.mult))
    step.wait()
    step.done(nc.vector.tensor_reduce(sums[:, :], comb[:, :, :], AX, ALU.add))
    step.wait()
    step.done(nc.vector.reciprocal(sums[:, :], sums[:, :]))
    step.wait()
    return nc.vector.tensor_tensor(comb[:, :, :], comb[:, :, :], bc(sums[:, :], 2, E), ALU.mult)


RANK_STEPS = 8


def attention0(nc, x, consts, w_attn, ctx_rows, ctx_cols, mask, X, xh, xl, K, ps, comb_dram):
    ctx = ExitStack()
    semaphores = []
    with ctx:
        def sb(name, shape, dt=F32):
            return ctx.enter_context(nc.sbuf_tensor("a_" + name, shape, dt))

        def slots(name, shape, dt=F32):
            return [sb(f"{name}{s}", shape, dt) for s in range(2)]

        def sem(name):
            semaphores.append(nc.alloc_semaphore("a_" + name))
            return semaphores[-1]

        W = sb("W", [P, C, A_ALL])
        idb = sb("idb", [P, P], BF16)
        causal = sb("causal", [P, SEQ], BF16)
        half = sb("half", [P, 2])
        mask4 = sb("mask4", [P, TILES, SEQ // 4], mybir.dt.int32)
        mask8 = mask4[:].bitcast(U8)
        maskf = sb("maskf", [P, TILES, P])
        maskneg = sb("maskneg", [P, TILES, P])
        logits = sb("logits", [P, TILES, E0])
        scores = sb("scores", [P, TILES, E0])
        comb = sb("comb", [P, TILES, E0])
        cmp = sb("cmp", [P, TILES * E0 * E0])
        eq = sb("eq", [P, TILES * E0 * E0])
        rank = sb("rank", [P, TILES * E0])
        sums = sb("sums", [P, TILES])
        combT = sb("combT", [E0 + SHARED0, TOKENS])

        stats = slots("stats", [P, 6])
        seen = slots("seen", [P, 6])
        mv = slots("mv", [P, 2])
        veps = slots("veps", [P, 1])
        rstd = slots("rstd", [P, 1])
        xt = slots("xt", [P, D])
        xn = slots("xn", [P, D])
        xT = slots("xT", [P, C, P])
        rot = slots("rot", [P, 512])
        qk = slots("qk", [P, 512])
        Vbd = slots("Vbd", [P, B2, PAIRS, 2 * HD])
        qT = slots("qT", [P, C, P])
        Kbd = slots("Kbd", [P, C, B2, CH * SEQ])
        mx = slots("mx", [P, HEADS])
        e = slots("e", [P, HEADS, SEQ])
        rs = slots("rs", [P, HEADS])
        PT = slots("PT", [P, PAIRS, P])
        aT = slots("aT", [P, C, P])
        memT = slots("memT", [P, C, P])
        mem = slots("mem", [P, D])
        xs = slots("xs", [P, P])
        xm = slots("xm", [P, 2])
        xp = slots("xp", [P, P])
        xPT = slots("xPT", [P, P])

        loaded = sem("loaded")
        ctx_loaded = [sem(f"ctx_loaded{s}") for s in range(2)]
        set_up = sem("set_up")
        bufs_set = sem("bufs_set")
        maskf_set = sem("maskf_set")
        low_ready = sem("low_ready")
        rank_step = sem("rank_step")
        sig_step = sem("sig_step")
        clamped = sem("clamped")
        dve_step = sem("dve_step")
        var_ready = sem("var_ready")
        rstd_ready = sem("rstd_ready")
        xn_ready = sem("xn_ready")
        xn_turned = sem("xn_turned")
        xT_ready = sem("xT_ready")
        qk_ready = sem("qk_ready")
        v_ready = sem("v_ready")
        rope_ready = sem("rope_ready")
        v_placed = sem("v_placed")
        qT_turned = sem("qT_turned")
        kT_turned = sem("kT_turned")
        qT_ready = sem("qT_ready")
        k_placed = sem("k_placed")
        scored = sem("scored")
        shifted = sem("shifted")
        exp_ready = sem("exp_ready")
        rs_ready = sem("rs_ready")
        probs_ready = sem("probs_ready")
        pT_turned = [sem(f"pT_turned{h}") for h in range(2)]
        pT_ready = [sem(f"pT_ready{h}") for h in range(2)]
        pv_ready = sem("pv_ready")
        aT_ready = sem("aT_ready")
        attn_ready = sem("attn_ready")
        x_scored = sem("x_scored")
        x_max_ready = sem("x_max_ready")
        x_exp_ready = sem("x_exp_ready")
        x_probs_ready = sem("x_probs_ready")
        x_pT_turned = sem("x_pT_turned")
        x_pT_ready = sem("x_pT_ready")
        read_out = sem("read_out")
        xh_ready = sem("xh_ready")
        logits_ready = sem("logits_ready")
        logits_kept = sem("logits_kept")
        sig_ready = sem("sig_ready")
        comb_ready = sem("comb_ready")
        comb_turned = sem("comb_turned")
        combT_ready = sem("combT_ready")
        comb_stored = sem("comb_stored")

        block = ctx.enter_context(nc.Block())
        ident = K[:, K_ID:K_ID + P]

        @block.sync
        def _(sp):
            sp.dma_start(K[:], consts).then_inc(loaded, 16)
            sp.dma_start(X[:], x).then_inc(loaded, 16)
            sp.dma_start(W[:], w_attn).then_inc(loaded, 16)
            for b in range(B2):
                sp.dma_start(mask4[b * SEQ:(b + 1) * SEQ], bc(mask[b], 0, SEQ)).then_inc(loaded, 16)

            def load_ctx(i, s):
                sp.dma_start(memT[s][:], ctx_cols[i * 2 + s]).then_inc(ctx_loaded[s], 16)
                sp.dma_start(mem[s][:], ctx_rows[i * 2 + s]).then_inc(ctx_loaded[s], 16)

            for s in range(2):
                load_ctx(0, s)
            with sp.Fori(1, TILES // 2) as i:
                for s in range(2):
                    sp.wait_ge(read_out, i * 2 + s - 1)
                    load_ctx(i, s)
            sp.wait_ge(combT_ready, 2)
            sp.dma_start(comb_dram, combT[:]).then_inc(comb_stored, 16)
            sp.wait_ge(comb_stored, 16)

        @block.gpsimd
        def _(pool):
            nc.gpsimd.memset(half[:], -0.5)
            for s in range(2):
                last = nc.gpsimd.memset(Vbd[s][:], 0.0)
            last.then_inc(bufs_set, 1)
            pool.wait_ge(bufs_set, 1)
            with pool.Fori(0, TILES // 2) as i:
                for k in range(3):
                    for s in range(2):
                        pool.wait_ge(var_ready, i * 6 + 2 * k + s + 1)
                        nc.gpsimd.tensor_tensor(rstd[s][:], veps[s][:], half[:, 0:1], ALU.pow).then_inc(rstd_ready, 1)
                    if k == 0:
                        for s in range(2):
                            pool.wait_ge(exp_ready, i * 2 + s + 1)
                            pool.wait_ge(rs_ready, i * 2 + s + 1)
                            nc.gpsimd.tensor_tensor(e[s][:], e[s][:], bc(rs[s][:], 2, SEQ), ALU.mult).then_inc(probs_ready, 1)

        @block.vector
        def _(dve):
            step = Steps(dve, dve_step, 28)
            dve.wait_ge(loaded, 16 * (3 + B2))
            nc.vector.tensor_copy(idb[:], ident)
            nc.vector.memset(maskf[:], 0.0).then_inc(maskf_set, 1)
            dve.wait_ge(maskf_set, 1)
            for b in range(B2):
                rows = slice(b * SEQ, (b + 1) * SEQ)
                nc.vector.tensor_copy(maskf[rows, :, rows], mask8[rows]).then_inc(maskf_set, 1)
            nc.vector.tensor_copy(causal[:], K[:, K_CAUSAL:K_CAUSAL + SEQ])
            nc.vector.memset(combT[:], 1.0)
            dve.wait_ge(maskf_set, 1 + B2)
            nc.vector.tensor_scalar(maskneg[:], maskf[:], 1.0, -NEG, ALU.subtract, ALU.mult).then_inc(set_up, 1)
            dve.wait_ge(set_up, 1)

            def normalise(i, s, k):
                step.done(nc.vector.bn_stats(stats[s][:], xt[s][:]))
                step.wait()
                nc.vector.tensor_copy(seen[s][:], stats[s][:])
                step.done(nc.vector.bn_aggr(mv[s][:], stats[s][:]))
                step.wait()
                nc.vector.tensor_scalar(veps[s][:], mv[s][:, 1:2], EPS, None, ALU.add).then_inc(var_ready, 1)

            def apply_norm(i, s, k):
                t = i * 2 + s
                dve.wait_ge(rstd_ready, i * 6 + 2 * k + s + 1)
                nc.vector.tensor_scalar(xn[s][:], xt[s][:], mv[s][:, 0:1], rstd[s][:], ALU.subtract, ALU.mult).then_inc(xn_ready, 1)

            def rope(i, s):
                dve.wait_ge(qk_ready, i * 2 + s + 1)
                q3 = ps[:, 4 * s + 1, :].rearrange("p (h d) -> p h d", d=HD)
                nc.vector.tensor_tensor(qk[s][:].rearrange("p (h d) -> p h d", d=HD), q3,
                                        bc(K[:, K_COS:K_COS + HD], 1, 2 * HEADS), ALU.mult)
                q4 = ps[:, 4 * s + 1, :].rearrange("p (h d e) -> p h d e", d=HD // 2, e=2)
                sin = bc(K[:, K_SIN0:K_SIN0 + HD], 1, 2 * HEADS).rearrange("p h (d e) -> p h d e", e=2)
                r4 = rot[s][:].rearrange("p (h d e) -> p h d e", d=HD // 2, e=2)
                step.done(nc.vector.tensor_tensor(r4, q4[:, :, :, ::-1], sin, ALU.mult))
                step.wait()
                nc.vector.tensor_tensor(qk[s][:], qk[s][:], rot[s][:], ALU.add).then_inc(rope_ready, 1)

            def place_k(i, s):
                dve.wait_ge(kT_turned, i * 2 + s + 1)
                kT = ps[:, 4 * s + 3, 0:2 * P].rearrange("p (c b k) -> p c b k", c=C, b=B2)
                for c in range(C):
                    ins = nc.vector.tensor_tensor(
                        Kbd[s][:, c].rearrange("p b (h k) -> p b h k", h=CH), bc(kT[:, c], 2, CH),
                        bc(bc(K[:, K_H16:K_H16 + CH], 1, B2), 3, SEQ), ALU.mult)
                ins.then_inc(k_placed, 1)

            def shift(i, s):
                dve.wait_ge(scored, i * 2 + s + 1)
                sc = ps[:, 4 * s + 1:4 * s + 3, :].rearrange("p c (h k) -> p (c h) k", k=SEQ)
                step.done(nc.vector.tensor_reduce(mx[s][:], sc, AX, ALU.max))
                step.wait()
                nc.vector.tensor_tensor(e[s][:], sc, bc(mx[s][:], 2, SEQ), ALU.subtract).then_inc(shifted, 1)

            def row_sums(i, s):
                dve.wait_ge(exp_ready, i * 2 + s + 1)
                step.done(nc.vector.tensor_reduce(rs[s][:], e[s][:], AX, ALU.add))
                step.wait()
                nc.vector.reciprocal(rs[s][:], rs[s][:]).then_inc(rs_ready, 1)

            def keep_pT(i, s):
                dve.wait_ge(pT_turned[1], i * 2 + s + 1)
                nc.vector.tensor_copy(PT[s][:, 4:8, :], ps[:, 4 * s + 3, :].rearrange("p (h q) -> p h q", h=4)).then_inc(pT_ready[1], 1)

            def add_attention(i, s):
                t = i * 2 + s
                dve.wait_ge(attn_ready, i * 2 + s + 1)
                step.done(nc.vector.tensor_tensor(xt[s][:], ps[:, 4 * s + 2, 0:D], X[:, t, :], ALU.add))
                step.wait()

            def x_shift(i, s):
                t = i * 2 + s
                dve.wait_ge(x_scored, i * 2 + s + 1)
                step.done(nc.vector.scalar_tensor_tensor(out=xs[s][:], in0=ps[:, 4 * s + 1, 0:P], scalar=float(D) ** -0.5,
                                                         in1=maskneg[:, t, :], op0=ALU.mult, op1=ALU.add))
                step.wait()
                nc.vector.tensor_reduce(xm[s][:, 0:1], xs[s][:], AX, ALU.max, negate=True).then_inc(x_max_ready, 1)

            def x_probs(i, s):
                t = i * 2 + s
                dve.wait_ge(x_exp_ready, i * 2 + s + 1)
                step.done(nc.vector.reciprocal(xm[s][:, 1:2], xm[s][:, 1:2]))
                step.wait()
                nc.vector.scalar_tensor_tensor(out=xp[s][:], in0=xs[s][:], scalar=xm[s][:, 1:2], in1=maskf[:, t, :],
                                               op0=ALU.mult, op1=ALU.mult).then_inc(x_probs_ready, 1)

            def add_read_out(i, s):
                t = i * 2 + s
                dve.wait_ge(read_out, i * 2 + s + 1)
                nc.vector.tensor_tensor(X[:, t, :], ps[:, 4 * s + 2, 0:D], xt[s][:], ALU.add)
                step.done(nc.vector.tensor_tensor(xt[s][:], ps[:, 4 * s + 2, 0:D], xt[s][:], ALU.add))
                step.wait()

            def low_part(i, s):
                t = i * 2 + s
                dve.wait_ge(xh_ready, i * 2 + s + 1)
                nc.vector.tensor_tensor(xl[:, :, bass.ds(t * P, P)], xT[s][:], xh[:, :, bass.ds(t * P, P)].bitcast(F32),
                                        ALU.subtract).then_inc(low_ready, 1)

            with dve.Fori(0, TILES // 2) as i:
                step.start(i)
                for s in range(2):
                    step.done(nc.vector.tensor_copy(xt[s][:], X[:, i * 2 + s, :]))
                    step.wait()
                    normalise(i, s, 0)
                for s in range(2):
                    apply_norm(i, s, 0)
                for s in range(2):
                    rope(i, s)
                for s in range(2):
                    place_k(i, s)
                for s in range(2):
                    shift(i, s)
                for s in range(2):
                    row_sums(i, s)
                for s in range(2):
                    keep_pT(i, s)
                for s in range(2):
                    add_attention(i, s)
                    normalise(i, s, 1)
                for s in range(2):
                    apply_norm(i, s, 1)
                for s in range(2):
                    x_shift(i, s)
                for s in range(2):
                    x_probs(i, s)
                for s in range(2):
                    add_read_out(i, s)
                    normalise(i, s, 2)
                for s in range(2):
                    apply_norm(i, s, 2)
                for s in range(2):
                    low_part(i, s)
                step.end()

            dve.wait_ge(logits_kept, TILES)
            nc.vector.tensor_scalar(logits[:], logits[:], -88.7, None, ALU.max).then_inc(clamped, 1)
            dve.wait_ge(sig_ready, 1)
            sstep = Steps(dve, sig_step, 2)
            sstep.start(0)
            sstep.done(nc.vector.tensor_scalar(scores[:], scores[:], 1.0, None, ALU.add))
            sstep.wait()
            sstep.done(nc.vector.reciprocal(scores[:], scores[:]))
            sstep.wait()
            rstep = Steps(dve, rank_step, RANK_STEPS)
            rstep.start(0)
            rank_and_combine(nc, dve, rstep, scores, K[:, K_TRI0:K_TRI0 + E0 * E0], E0, TOP0,
                             cmp, eq, rank, sums, comb).then_inc(comb_ready, 1)
            dve.wait_ge(comb_turned, 1)
            for n in range(2):
                nc.vector.tensor_copy(combT[0:E0, n * 512:(n + 1) * 512], ps[0:E0, n, :]).then_inc(combT_ready, 1)

        @block.scalar
        def _(act):
            def keep_xT(i, s, k):
                act.wait_ge(xn_turned, i * 6 + 2 * k + s + 1)
                nc.scalar.copy(xT[s][:], ps[:, 4 * s, 0:D].rearrange("p (c t) -> p c t", c=C)).then_inc(xT_ready, 1)

            def place_v(i, s):
                act.wait_ge(v_ready, i * 2 + s + 1)
                for h in range(2):
                    at = slice(h * SEQ, (h + 1) * SEQ)
                    src = ps[at, 4 * s + 2, 0:B2 * P].rearrange("p (b n d) -> p b n d", b=B2, n=PAIRS)
                    ins = nc.scalar.copy(Vbd[s][at, :, :, h * HD:(h + 1) * HD], src)
                ins.then_inc(v_placed, 1)

            def keep_qT(i, s):
                act.wait_ge(qT_turned, i * 2 + s + 1)
                nc.scalar.copy(qT[s][:], ps[:, 4 * s, 0:D].rearrange("p (c t) -> p c t", c=C)).then_inc(qT_ready, 1)

            def exps(i, s):
                act.wait_ge(shifted, i * 2 + s + 1)
                nc.scalar.activation(e[s][:], e[s][:], ACT.Exp, scale=float(HD) ** -0.5).then_inc(exp_ready, 1)

            def keep_pT(i, s):
                act.wait_ge(pT_turned[0], i * 2 + s + 1)
                nc.scalar.copy(PT[s][:, 0:4, :], ps[:, 4 * s, :].rearrange("p (h q) -> p h q", h=4)).then_inc(pT_ready[0], 1)

            def keep_aT(i, s):
                act.wait_ge(pv_ready, i * 2 + s + 1)
                nc.scalar.copy(aT[s][:], ps[:, 4 * s + 1, 0:D].rearrange("p (c t) -> p c t", c=C)).then_inc(aT_ready, 1)

            def x_exps(i, s):
                act.wait_ge(x_max_ready, i * 2 + s + 1)
                nc.scalar.activation(xs[s][:], xs[s][:], ACT.Exp, bias=xm[s][:, 0:1], accum_out=xm[s][:, 1:2]).then_inc(x_exp_ready, 1)

            def x_keep_pT(i, s):
                act.wait_ge(x_pT_turned, i * 2 + s + 1)
                nc.scalar.copy(xPT[s][:], ps[:, 4 * s + 3, 0:P]).then_inc(x_pT_ready, 1)

            def high_part(i, s):
                t = i * 2 + s
                act.wait_ge(xT_ready, i * 6 + 4 + s + 1)
                nc.scalar.copy(xh[:, :, bass.ds(t * P, P)], xT[s][:]).then_inc(xh_ready, 1)

            def keep_logits(i, s):
                t = i * 2 + s
                act.wait_ge(logits_ready, i * 2 + s + 1)
                nc.scalar.copy(logits[:, t, :], ps[:, 4 * s + 1, 0:E0]).then_inc(logits_kept, 1)

            act.wait_ge(bufs_set, 1)
            with act.Fori(0, TILES // 2) as i:
                for s in range(2):
                    keep_xT(i, s, 0)
                for s in range(2):
                    place_v(i, s)
                for s in range(2):
                    keep_qT(i, s)
                for s in range(2):
                    exps(i, s)
                for s in range(2):
                    keep_pT(i, s)
                for s in range(2):
                    keep_aT(i, s)
                for s in range(2):
                    keep_xT(i, s, 1)
                for s in range(2):
                    x_exps(i, s)
                for s in range(2):
                    x_keep_pT(i, s)
                for s in range(2):
                    keep_xT(i, s, 2)
                    high_part(i, s)
                for s in range(2):
                    keep_logits(i, s)
            act.wait_ge(clamped, 1)
            nc.scalar.activation(scores[:], logits[:], ACT.Exp, scale=-1.0).then_inc(sig_ready, 1)

        @block.tensor
        def _(pe):
            def turn_xn(i, s, k):
                pe.wait_ge(xn_ready, i * 6 + 2 * k + s + 1)
                for c in range(C):
                    mm = nc.tensor.transpose(ps[:, 4 * s, c * P:(c + 1) * P], xn[s][:, c * P:(c + 1) * P], ident)
                mm.then_inc(xn_turned, 1)

            def project(i, s):
                pe.wait_ge(xT_ready, i * 6 + s + 1)
                for c in range(C):
                    mm = nc.tensor.matmul(ps[:, 4 * s + 1, :], xT[s][:, c, :], W[:, c, A_QK:A_QK + 512],
                                          start=(c == 0), stop=(c == C - 1))
                mm.then_inc(qk_ready, 1)
                for b in range(B2):
                    for h in range(2):
                        rows = slice(h * SEQ, (h + 1) * SEQ)
                        for c in range(C):
                            wv = W[:, c, A_V:A_V + D].rearrange("p (n h d) -> p n h d", h=2, d=HD)[:, :, h, :]
                            mm = nc.tensor.matmul(ps[rows, 4 * s + 2, b * P:(b + 1) * P].rearrange("p (n d) -> p n d", d=HD),
                                                  xT[s][:, c, b * SEQ:(b + 1) * SEQ], wv, start=(c == 0), stop=(c == C - 1))
                mm.then_inc(v_ready, 1)

            def turn_qk(i, s):
                pe.wait_ge(rope_ready, i * 2 + s + 1)
                for n, (bank, done) in enumerate([(0, qT_turned), (3, kT_turned)]):
                    for c in range(C):
                        at = n * D + c * P
                        mm = nc.tensor.transpose(ps[:, 4 * s + bank, c * P:(c + 1) * P], qk[s][:, at:at + P], ident)
                    mm.then_inc(done, 1)

            def score(i, s):
                pe.wait_ge(v_placed, i * 2 + s + 1)
                pe.wait_ge(qT_ready, i * 2 + s + 1)
                pe.wait_ge(k_placed, i * 2 + s + 1)
                for c in range(C):
                    bank = ps[:, 4 * s + 1 + c, :]
                    nc.tensor.matmul(bank.rearrange("p (h k) -> p h k", k=SEQ), idb[:], bc(causal[:], 1, CH),
                                     start=True, stop=False, skip_group_check=True)
                    for b in range(B2):
                        rows = slice(b * SEQ, (b + 1) * SEQ)
                        mm = nc.tensor.matmul(ps[rows, 4 * s + 1 + c, :], qT[s][:, c, rows], Kbd[s][:, c, b, :],
                                              start=False, stop=True, skip_group_check=True)
                mm.then_inc(scored, 1)

            def turn_probs(i, s):
                pe.wait_ge(probs_ready, i * 2 + s + 1)
                for h in range(2):
                    for n in range(4):
                        mm = nc.tensor.transpose(ps[:, 4 * s + 3 * h, n * P:(n + 1) * P],
                                                 e[s][:, 8 * h + 2 * n:8 * h + 2 * n + 2, :].rearrange("p h k -> p (h k)"), ident)
                    mm.then_inc(pT_turned[h], 1)

            def weigh_values(i, s):
                for h in range(2):
                    pe.wait_ge(pT_ready[h], i * 2 + s + 1)
                for n in range(PAIRS):
                    for b in range(B2):
                        r = 32 * (n % 4)
                        mm = nc.tensor.matmul(ps[r:r + 32, 4 * s + 1, (n // 4) * P + b * SEQ:(n // 4) * P + (b + 1) * SEQ],
                                              Vbd[s][:, b, n, :], PT[s][:, n, b * SEQ:(b + 1) * SEQ], start=True, stop=True,
                                              tile_position=(0, r))
                mm.then_inc(pv_ready, 1)

            def project_out(i, s):
                pe.wait_ge(aT_ready, i * 2 + s + 1)
                for c in range(C):
                    mm = nc.tensor.matmul(ps[:, 4 * s + 2, 0:D], aT[s][:, c, :], W[:, c, A_O:A_O + D],
                                          start=(c == 0), stop=(c == C - 1))
                mm.then_inc(attn_ready, 1)

            def x_score(i, s):
                pe.wait_ge(xT_ready, i * 6 + 2 + s + 1)
                pe.wait_ge(ctx_loaded[s], (i + 1) * 32)
                for c in range(C):
                    mm = nc.tensor.matmul(ps[:, 4 * s + 1, 0:P], xT[s][:, c, :], memT[s][:, c, :],
                                          start=(c == 0), stop=(c == C - 1))
                mm.then_inc(x_scored, 1)

            def x_turn_probs(i, s):
                pe.wait_ge(x_probs_ready, i * 2 + s + 1)
                nc.tensor.transpose(ps[:, 4 * s + 3, 0:P], xp[s][:], ident).then_inc(x_pT_turned, 1)

            def x_read_out(i, s):
                pe.wait_ge(x_pT_ready, i * 2 + s + 1)
                nc.tensor.matmul(ps[:, 4 * s + 2, 0:D], xPT[s][:], mem[s][:], start=True, stop=True).then_inc(read_out, 1)

            def route(i, s):
                pe.wait_ge(xT_ready, i * 6 + 4 + s + 1)
                for c in range(C):
                    mm = nc.tensor.matmul(ps[:, 4 * s + 1, 0:E0], xT[s][:, c, :], W[:, c, A_R:A_R + E0],
                                          start=(c == 0), stop=(c == C - 1))
                mm.then_inc(logits_ready, 1)

            pe.wait_ge(loaded, 16 * (3 + B2))
            pe.wait_ge(set_up, 1)
            with pe.Fori(0, TILES // 2) as i:
                for s in range(2):
                    turn_xn(i, s, 0)
                for s in range(2):
                    project(i, s)
                for s in range(2):
                    turn_qk(i, s)
                for s in range(2):
                    score(i, s)
                for s in range(2):
                    turn_probs(i, s)
                for s in range(2):
                    weigh_values(i, s)
                for s in range(2):
                    project_out(i, s)
                for s in range(2):
                    turn_xn(i, s, 1)
                for s in range(2):
                    x_score(i, s)
                for s in range(2):
                    x_turn_probs(i, s)
                for s in range(2):
                    x_read_out(i, s)
                for s in range(2):
                    turn_xn(i, s, 2)
                for s in range(2):
                    route(i, s)
            pe.wait_ge(comb_ready, 1)
            for t in range(TILES):
                mm = nc.tensor.transpose(ps[0:E0, t // 4, (t % 4) * P:(t % 4 + 1) * P], comb[:, t, :], ident)
            mm.then_inc(comb_turned, 1)
    end_program(nc, semaphores)


def experts(nc, tag, w_dram, comb_dram, chunks, per_body, hidden, w_slots, h_slots, X, xh, xl, K, ps, out):
    ctx = ExitStack()
    semaphores = []
    bodies = chunks // per_body
    units = HALVES * chunks
    LEAD = 2
    LAG = 2
    GU = 2 * C * P
    WC = GU + D
    parts = []
    for j in range(per_body):
        row, end, of = j * P, (j + 1) * P, []
        while row < end:
            n = min(end, (row // hidden + 1) * hidden) - row
            of.append((row // hidden, row - j * P, n))
            row += n
        parts.append(of)
    per_expert = hidden % P == 0
    comb_slots = per_body * P // hidden if per_expert else per_body
    experts_in_body = per_body * P // hidden
    with ctx:
        def sb(name, shape, dt=F32):
            return ctx.enter_context(nc.sbuf_tensor(f"{tag}_{name}", shape, dt))

        def sem(name):
            semaphores.append(nc.alloc_semaphore(f"{tag}_{name}"))
            return semaphores[-1]

        raw = [sb(f"raw{n}", [P, WC]) for n in range(w_slots)]
        wh = [sb(f"wh{n}", [P, WC], F32R) for n in range(w_slots)]
        wl = [sb(f"wl{n}", [P, WC], F32R) for n in range(w_slots)]
        cb = [sb(f"cb{n}", [P, TOKENS]) for n in range(comb_slots)]
        act_out = [sb(f"act{n}", [P, HT]) for n in range(2)]
        hu = [sb(f"hu{n}", [P, HT]) for n in range(2)]
        h = [sb(f"h{n}", [P, HT]) for n in range(h_slots)]
        hh = [sb(f"hh{n}", [P, HT], F32R) for n in range(h_slots)]
        hl = [sb(f"hl{n}", [P, HT], F32R) for n in range(h_slots)]
        zeros = sb("zeros", [P, HT], BF16)
        oT = [[sb(f"oT{c}{t}", [P, HT]) for t in range(HALVES)] for c in range(C)]

        w_loaded = [sem(f"w_loaded{n}") for n in range(w_slots)]
        cb_loaded = [sem(f"cb_loaded{n}") for n in range(comb_slots)]
        zeros_set = sem("zeros_set")
        wh_ready = sem("wh_ready")
        wl_ready = sem("wl_ready")
        gate_ready = sem("gate_ready")
        up_ready = sem("up_ready")
        silu_ready = sem("silu_ready")
        hu_ready = sem("hu_ready")
        h_ready = sem("h_ready")
        hh_ready = sem("hh_ready")
        hl_ready = sem("hl_ready")
        down_done = sem("down_done")
        sum_done = sem("sum_done")
        oT_act = sem("oT_act")
        oT_dve = sem("oT_dve")
        turned = sem("turned")
        x_added = sem("x_added")
        stored = sem("stored")

        block = ctx.enter_context(nc.Block())
        ident = K[:, K_ID:K_ID + P]
        acc = [[ps[:, 4 + 2 * c + t, :] for t in range(HALVES)] for c in range(C)]

        def load_weights(eng, i, j):
            n = j % w_slots
            if not (isinstance(i, int) and i == 0 and j < w_slots):
                eng.wait_ge(wh_ready, i * per_body + j - w_slots + 1)
                eng.wait_ge(wl_ready, i * per_body + j - w_slots + 1)
            eng.dma_start(raw[n][:], w_dram[i * per_body + j]).then_inc(w_loaded[n], 16)

        def load_comb(eng, i, j):
            if per_expert:
                if j * P % hidden:
                    return
                slot, of = j * P // hidden, [(j * P // hidden, 0, P)]
                last_unit = HALVES * (j + hidden // P)
            else:
                slot, of = j, parts[j]
                last_unit = HALVES * (j + 1)
            if not (isinstance(i, int) and i == 0):
                eng.wait_ge(h_ready, (i - 1) * HALVES * per_body + last_unit)
            for expert, row, n in of:
                eng.dma_start(cb[slot][row:row + n], bc(comb_dram[i * experts_in_body + expert], 0, n)).then_inc(cb_loaded[slot], 16)

        @block.sync
        def _(sp):
            def body(i):
                for j in range(per_body):
                    load_comb(sp, i, j)
                    load_weights(sp, i, j)

            body(0)
            with sp.Fori(1, bodies) as i:
                body(i)
            if out is not None:
                for t in range(TILES):
                    sp.wait_ge(x_added, t + 1)
                    sp.dma_start(out[:, t, :], X[:, t, :]).then_inc(stored, 16)
                sp.wait_ge(stored, 16 * TILES)

        @block.gpsimd
        def _(pool):
            def body(i):
                for u in range(HALVES * per_body):
                    j, t = u // HALVES, u % HALVES
                    unit = i * HALVES * per_body + u
                    slot = j * P // hidden if per_expert else j
                    if t == 0:
                        n = 1 if per_expert else len(parts[j])
                        pool.wait_ge(cb_loaded[slot], (i + 1) * 16 * n)
                    pool.wait_ge(hu_ready, unit + 1)
                    nc.gpsimd.tensor_tensor(h[u % h_slots][:], hu[u % 2][:], cb[slot][:, t * HT:(t + 1) * HT],
                                            ALU.mult).then_inc(h_ready, 1)

            body(0)
            with pool.Fori(1, bodies) as i:
                body(i)

        @block.scalar
        def _(act):
            def split(chunk, first, slot, rnd):
                act.wait_ge(w_loaded[slot], 16 * rnd)
                if not first:
                    act.wait_ge(down_done, (chunk - w_slots + 1) * HALVES)
                nc.scalar.copy(wh[slot][:], raw[slot][:]).then_inc(wh_ready, 1)

            def body(i, last):
                for u in range(HALVES * per_body):
                    j = u // HALVES
                    unit = i * HALVES * per_body + u
                    act.wait_ge(gate_ready, unit + 1)
                    if not (isinstance(i, int) and i == 0 and u < 2):
                        act.wait_ge(hu_ready, unit - 1)
                    nc.scalar.activation(act_out[u % 2][:], ps[:, 2 * (u % 2), :], ACT.Silu).then_inc(silu_ready, 1)
                    if not (isinstance(i, int) and i == 0 and u == 0):
                        high_h(unit - 1, (u - 1) % h_slots, isinstance(i, int) and i == 0 and u - 1 < h_slots)
                    if u % HALVES == 0 and not (last and j + LEAD >= per_body):
                        m = j + LEAD
                        split(i * per_body + m, isinstance(i, int) and i == 0 and m < w_slots, m % w_slots,
                              i * (per_body // w_slots) + m // w_slots + 1)

            def high_h(unit, slot, first):
                act.wait_ge(h_ready, unit + 1)
                if not first:
                    act.wait_ge(down_done, unit - h_slots + 1)
                nc.scalar.copy(hh[slot][:], h[slot][:]).then_inc(hh_ready, 1)

            for m in range(LEAD):
                split(m, True, m, 1)
            body(0, False)
            with act.Fori(1, bodies - 1) as i:
                body(i, False)
            body(bodies - 1, True)
            high_h(units - 1, (HALVES * per_body - 1) % h_slots, False)
            act.wait_ge(sum_done, 1)
            for t in range(HALVES):
                nc.scalar.copy(oT[0][t][:], acc[0][t]).then_inc(oT_act, 1)

        @block.vector
        def _(dve):
            def split(chunk, first, slot, rnd):
                dve.wait_ge(wh_ready, chunk + 1)
                nc.vector.tensor_tensor(wl[slot][:], raw[slot][:], wh[slot][:].bitcast(F32), ALU.subtract).then_inc(wl_ready, 1)

            def low_h(unit, slot):
                dve.wait_ge(hh_ready, unit + 1)
                nc.vector.tensor_tensor(hl[slot][:], h[slot][:], hh[slot][:].bitcast(F32), ALU.subtract).then_inc(hl_ready, 1)

            def body(i, last):
                for u in range(HALVES * per_body):
                    j = u // HALVES
                    unit = i * HALVES * per_body + u
                    dve.wait_ge(up_ready, unit + 1)
                    dve.wait_ge(silu_ready, unit + 1)
                    if not (isinstance(i, int) and i == 0 and u < 2):
                        dve.wait_ge(h_ready, unit - 1)
                    nc.vector.tensor_tensor(hu[u % 2][:], act_out[u % 2][:], ps[:, 2 * (u % 2) + 1, :], ALU.mult).then_inc(hu_ready, 1)
                    if not (isinstance(i, int) and i == 0 and u == 0):
                        low_h(unit - 1, (u - 1) % h_slots)
                    if u % HALVES == 1 and not (last and j + LEAD >= per_body):
                        m = j + LEAD
                        split(i * per_body + m, False, m % w_slots, None)

            nc.vector.memset(zeros[:], 0.0).then_inc(zeros_set, 1)
            for m in range(LEAD):
                split(m, True, m, 1)
            body(0, False)
            with dve.Fori(1, bodies - 1) as i:
                body(i, False)
            body(bodies - 1, True)
            low_h(units - 1, (HALVES * per_body - 1) % h_slots)
            dve.wait_ge(sum_done, 1)
            for t in range(HALVES):
                nc.vector.tensor_copy(oT[1][t][:], acc[1][t]).then_inc(oT_dve, 1)
            for t in range(TILES):
                dve.wait_ge(turned, t + 1)
                nc.vector.tensor_tensor(X[:, t, :], ps[:, t % 4, 0:D], X[:, t, :], ALU.add).then_inc(x_added, 1)

        @block.tensor
        def _(pe):
            def three(dst, hi, lo, rhs_hi, rhs_lo, first, last, **kw):
                nc.tensor.matmul(dst, hi, rhs_hi, start=first, stop=False, **kw)
                nc.tensor.matmul(dst, hi, rhs_lo, start=False, stop=False, **kw)
                return nc.tensor.matmul(dst, lo, rhs_hi, start=False, stop=last, **kw)

            def gate_up(i, u):
                j, t = u // HALVES, u % HALVES
                unit = i * HALVES * per_body + u
                w = j % w_slots
                tok = slice(t * HT, (t + 1) * HT)
                if t == 0:
                    pe.wait_ge(wh_ready, i * per_body + j + 1)
                    pe.wait_ge(wl_ready, i * per_body + j + 1)
                if not (isinstance(i, int) and i == 0 and u < 2):
                    pe.wait_ge(silu_ready, unit - 1)
                    pe.wait_ge(hu_ready, unit - 1)
                for n, done in ((0, gate_ready), (1, up_ready)):
                    for c in range(C):
                        at = slice((n * C + c) * P, (n * C + c + 1) * P)
                        mm = three(ps[:, 2 * (u % 2) + n, :], wh[w][:, at], wl[w][:, at], xh[:, c, tok], xl[:, c, tok],
                                   c == 0, c == C - 1)
                    mm.then_inc(done, 1)

            def down(unit, j, t, slot):
                w = j % w_slots
                pe.wait_ge(hh_ready, unit + 1)
                pe.wait_ge(hl_ready, unit + 1)
                for c in range(C):
                    at = slice(GU + c * P, GU + (c + 1) * P)
                    mm = three(acc[c][t], wh[w][:, at], wl[w][:, at], hh[slot][:], hl[slot][:], False, False,
                               skip_group_check=True)
                mm.then_inc(down_done, 1)

            def body(i):
                n = HALVES * per_body
                for u in range(n):
                    gate_up(i, u)
                    if not (isinstance(i, int) and i == 0 and u < LAG):
                        v = (u - LAG) % n
                        down(i * n + u - LAG, v // HALVES, v % HALVES, v % h_slots)

            pe.wait_ge(zeros_set, 1)
            for c in range(C):
                for t in range(HALVES):
                    nc.tensor.matmul(acc[c][t], zeros[:, 0:P], zeros[:], start=True, stop=False, skip_group_check=True)
            body(0)
            with pe.Fori(1, bodies) as i:
                body(i)
            for v in range(HALVES * per_body - LAG, HALVES * per_body):
                down((bodies - 1) * HALVES * per_body + v, v // HALVES, v % HALVES, v % h_slots)
            for c in range(C):
                for t in range(HALVES):
                    mm = nc.tensor.matmul(acc[c][t], zeros[:, 0:P], zeros[:], start=False, stop=True, skip_group_check=True)
            mm.then_inc(sum_done, 1)
            pe.wait_ge(oT_act, HALVES)
            pe.wait_ge(oT_dve, HALVES)
            for t in range(TILES):
                if t >= 4:
                    pe.wait_ge(x_added, t - 3)
                for c in range(C):
                    part = oT[c][t // 4][:, (t % 4) * P:(t % 4 + 1) * P]
                    mm = nc.tensor.transpose(ps[:, t % 4, c * P:(c + 1) * P], part, ident)
                mm.then_inc(turned, 1)
    end_program(nc, semaphores)


def attention1(nc, w_attn, ctx_rows, ctx_lhs, lam, bias, X, xh, xl, K, ps, ctx_dram, comb_dram):
    ctx = ExitStack()
    semaphores = []
    UNITS = B2 * JP
    BLK = 2 * KV
    SC = (HD // 2) ** -0.5
    XSC = 8.0 ** -0.5
    QROWS, KROWS = 96, 96 + G4
    RING = 4
    with ctx:
        def sb(name, shape, dt=F32):
            return ctx.enter_context(nc.sbuf_tensor("b_" + name, shape, dt))

        def slots(name, shape, dt=F32):
            return [sb(f"{name}{s}", shape, dt) for s in range(2)]

        def sem(name):
            semaphores.append(nc.alloc_semaphore("b_" + name))
            return semaphores[-1]

        W = sb("W", [P, C, W_ALL])
        idb = sb("idb", [P, P], BF16)
        causal = sb("causal", [P, SEQ], BF16)
        half = sb("half", [P, 2])
        lamt = sb("lamt", [P, JP, KV])
        biast = sb("biast", [P, E1])
        logits = sb("logits", [P, TILES, E1])
        scores = sb("scores", [P, TILES, E1])
        comb = sb("comb", [P, TILES, E1])
        cmp = sb("cmp", [P, TILES * E1 * E1])
        eq = sb("eq", [P, TILES * E1 * E1])
        rank = sb("rank", [P, TILES * E1])
        sums = sb("sums", [P, TILES])
        combT = sb("combT", [E1, TOKENS])

        stats = slots("stats", [P, 6])
        seen = slots("seen", [P, 6])
        mv = slots("mv", [P, 2])
        veps = slots("veps", [P, 1])
        rstd = slots("rstd", [P, 1])
        xt = slots("xt", [P, D])
        xn = slots("xn", [P, D])
        xT = slots("xT", [P, C, P])
        rot = slots("rot", [P, 320])
        qk = slots("qk", [P, 320])
        qT = slots("qT", [SEQ, B2, JP, 2, SEQ])
        Kbd = slots("Kbd", [SEQ, B2, BLK, SEQ])
        Vbd = slots("Vbd", [P, B2, 2, 2 * HD])
        mx = slots("mx", [P, UNITS * BLK])
        e = slots("e", [P, UNITS, KV, 2, SEQ])
        w = slots("w", [P, UNITS, KV, 2])
        d = slots("d", [P, UNITS, KV, SEQ])
        dsum = slots("dsum", [P, UNITS * KV])
        PT = slots("PT", [P, UNITS, 2, P])
        aT = slots("aT", [P, C, P])
        xnh = slots("xnh", [P, D], F32R)
        xnl = slots("xnl", [P, D], F32R)
        craw = sb("craw", [P, TILES, D])
        chigh = sb("chigh", [P, TILES, D], F32R)
        clow = sb("clow", [P, TILES, D], F32R)
        Q = slots("Q", [KROWS, SB, D], F32R)
        Cx = slots("Cx", [KROWS, SB, G4, D], F32R)
        smax = slots("smax", [P, G4, SB, C])
        rowmax = slots("rowmax", [G4 * SB * C, P], F32R)
        vraw = slots("vraw", [P, C, GT * 8])
        VT = slots("VT", [P, C, GT, 9])
        PX = [slots(f"PX{n}", [P, C, D]) for n in range(RING)]
        rden = slots("rden", [P, C * GT])
        ret = slots("ret", [P, C, P])

        loaded = sem("loaded")
        set_up = sem("set_up")
        bufs_set = sem("bufs_set")
        dve_step = sem("dve_step")
        pool_step = sem("pool_step")
        var_ready = sem("var_ready")
        rstd_ready = sem("rstd_ready")
        xn_ready = sem("xn_ready")
        xn_turned = sem("xn_turned")
        xT_ready = sem("xT_ready")
        qk_ready = sem("qk_ready")
        v_ready = sem("v_ready")
        rope_ready = sem("rope_ready")
        v_placed = sem("v_placed")
        qT_turned = sem("qT_turned")
        kT_turned = sem("kT_turned")
        qT_ready = sem("qT_ready")
        k_placed = sem("k_placed")
        scored = sem("scored")
        shifted = sem("shifted")
        exp_ready = sem("exp_ready")
        w_ready = sem("w_ready")
        diff_ready = sem("diff_ready")
        relu_ready = sem("relu_ready")
        dsum_ready = sem("dsum_ready")
        probs_ready = sem("probs_ready")
        pT_turned = [sem(f"pT_turned{h}") for h in range(2)]
        pT_ready = [sem(f"pT_ready{h}") for h in range(2)]
        pv_ready = sem("pv_ready")
        aT_ready = sem("aT_ready")
        attn_ready = sem("attn_ready")
        ctx_loaded = [sem(f"ctx_loaded{s}") for s in range(2)]
        ctx_high = sem("ctx_high")
        ctx_low = sem("ctx_low")
        ctx_stored = sem("ctx_stored")
        craw_loaded = sem("craw_loaded")
        ctx_placed = [sem(f"ctx_placed{s}") for s in range(2)]
        vt_ready = sem("vt_ready")
        xn_high = sem("xn_high")
        xn_low = sem("xn_low")
        q_placed = [sem(f"q_placed{s}") for s in range(2)]
        s_ready = sem("s_ready")
        s_max = sem("s_max")
        max_turned = sem("max_turned")
        max_high = sem("max_high")
        max_placed = [sem(f"max_placed{s}") for s in range(2)]
        st_ready = sem("st_ready")
        px_ready = sem("px_ready")
        pvx_done = sem("pvx_done")
        ret_ready = sem("ret_ready")
        ret_turned = sem("ret_turned")
        xh_ready = sem("xh_ready")
        low_ready = sem("low_ready")
        logits_ready = sem("logits_ready")
        logits_kept = sem("logits_kept")
        soft_step = sem("soft_step")
        l_shifted = sem("l_shifted")
        l_exp = sem("l_exp")
        rank_step = sem("rank_step")
        comb_ready = sem("comb_ready")
        comb_turned = sem("comb_turned")
        combT_ready = sem("combT_ready")
        comb_stored = sem("comb_stored")

        block = ctx.enter_context(nc.Block())
        ident = K[:, K_ID:K_ID + P]
        PAIR_LOOP = TILES // 2
        SU = SB * C

        @block.sync
        def _(sp):
            sp.dma_start(W[:], w_attn).then_inc(loaded, 16)
            sp.dma_start(biast[:], bc(bias, 0, P)).then_inc(loaded, 16)
            for jj in range(2):
                sp.dma_start(lamt[jj * SEQ:(jj + 1) * SEQ], bc(lam[jj], 0, SEQ)).then_inc(loaded, 16)

            def load_v(t, s):
                sp.dma_start(vraw[s][:], ctx_lhs[t]).then_inc(ctx_loaded[s], 16)

            def place_ctx(t, s):
                for n, part in enumerate((0, 1, 0)):
                    for g in range(G4):
                        rows = slice(32 * n + 8 * g, 32 * n + 8 * g + 8)
                        src = ctx_dram[part, t].rearrange("(b g r) n -> g r b n", b=SB, g=G4)[g]
                        sp.dma_start(Cx[s][rows, :, g, :].bitcast(F32), src).then_inc(ctx_placed[s], 16)

            def place_q(i, s):
                sp.wait_ge(xn_high, i * 2 + s + 1)
                sp.wait_ge(xn_low, i * 2 + s + 1)
                for n, src in enumerate((xnh[s], xnh[s], xnl[s])):
                    for b in range(SB):
                        sp.dma_start(Q[s][32 * n:32 * n + 32, b, :].bitcast(F32), src[32 * b:32 * b + 32].bitcast(F32)).then_inc(q_placed[s], 16)

            def place_max(i, s):
                sp.wait_ge(max_high, i * 2 + s + 1)
                n = SB * C
                for g in range(G4):
                    dst = Q[s][QROWS + g:QROWS + g + 1].rearrange("p b (c m) -> p (b c) m", c=C)
                    sp.dma_start(dst.bitcast(F32), rowmax[s][g * n:(g + 1) * n].bitcast(F32)).then_inc(max_placed[s], 16)

            def rest(i):
                for s in range(2):
                    place_q(i, s)
                for s in range(2):
                    place_max(i, s)

            sp.dma_start(craw[:], ctx_rows.rearrange("t p d -> p t d")).then_inc(craw_loaded, 16)
            for s in range(2):
                load_v(s, s)
            sp.wait_ge(ctx_high, 1)
            sp.dma_start(ctx_dram[0].rearrange("t p d -> p t d"), chigh[:].bitcast(F32)).then_inc(ctx_stored, 16)
            sp.wait_ge(ctx_low, 1)
            sp.dma_start(ctx_dram[1].rearrange("t p d -> p t d"), clow[:].bitcast(F32)).then_inc(ctx_stored, 16)
            sp.wait_ge(ctx_stored, 32)
            sp.wait_ge(bufs_set, 3)
            for s in range(2):
                place_ctx(s, s)
            rest(0)
            with sp.Fori(1, PAIR_LOOP) as i:
                for s in range(2):
                    sp.wait_ge(vt_ready, i * 2 + s - 1)
                    load_v(i * 2 + s, s)
                for s in range(2):
                    sp.wait_ge(ret_ready, i * 2 + s - 1)
                    place_ctx(i * 2 + s, s)
                rest(i)
            sp.wait_ge(combT_ready, 2)
            sp.dma_start(comb_dram, combT[:]).then_inc(comb_stored, 16)
            sp.wait_ge(comb_stored, 16)

        @block.gpsimd
        def _(pool):
            step = Steps(pool, pool_step, 4)
            nc.gpsimd.memset(half[:], -0.5)
            for s in range(2):
                nc.gpsimd.memset(Vbd[s][:], 0.0)
                nc.gpsimd.memset(VT[s][:], 1.0)
                last = nc.gpsimd.memset(Cx[s][:].bitcast(F32), 0.0)
            last.then_inc(bufs_set, 1)
            pool.wait_ge(bufs_set, 1)

            def rsqrt(i, s, k):
                pool.wait_ge(var_ready, i * 6 + 2 * k + s + 1)
                nc.gpsimd.tensor_tensor(rstd[s][:], veps[s][:], half[:, 0:1], ALU.pow).then_inc(rstd_ready, 1)

            def differences(i, s):
                for b in range(B2):
                    u = slice(b * JP, (b + 1) * JP)
                    pool.wait_ge(w_ready, (i * 2 + s) * B2 + b + 1)
                    eb = e[s][:, u].rearrange("p u g h k -> p (u g h) k")
                    step.done(nc.gpsimd.tensor_tensor(eb, eb, bc(w[s][:, u].rearrange("p u g h -> p (u g h)"), 2, SEQ), ALU.mult))
                    step.wait()
                    e4 = e[s][:, u].rearrange("p u g h k -> p (u g) h k")
                    nc.gpsimd.tensor_tensor(d[s][:, u].rearrange("p u g k -> p (u g) k"), e4[:, :, 0], e4[:, :, 1],
                                            ALU.subtract).then_inc(diff_ready, 1)

            def normalise_diff(i, s):
                for b in range(B2):
                    u = slice(b * JP, (b + 1) * JP)
                    pool.wait_ge(relu_ready, (i * 2 + s) * B2 + b + 1)
                    pool.wait_ge(dsum_ready, (i * 2 + s) * B2 + b + 1)
                    db = d[s][:, u].rearrange("p u g k -> p (u g) k")
                    nc.gpsimd.tensor_tensor(db, db, bc(dsum[s][:, b * JP * KV:(b + 1) * JP * KV], 2, SEQ), ALU.mult).then_inc(probs_ready, 1)

            with pool.Fori(0, PAIR_LOOP) as i:
                step.start(i)
                for s in range(2):
                    rsqrt(i, s, 0)
                for s in range(2):
                    differences(i, s)
                for s in range(2):
                    normalise_diff(i, s)
                for s in range(2):
                    rsqrt(i, s, 1)
                for s in range(2):
                    rsqrt(i, s, 2)
                step.end()

        @block.vector
        def _(dve):
            step = Steps(dve, dve_step, 42)
            dve.wait_ge(loaded, 64)
            dve.wait_ge(bufs_set, 1)
            nc.vector.tensor_copy(idb[:], ident).then_inc(set_up, 1)
            nc.vector.tensor_copy(causal[:], K[:, K_CAUSAL:K_CAUSAL + SEQ]).then_inc(set_up, 1)
            for s in range(2):
                for b in range(SB):
                    one = K[QROWS:KROWS, K_ONE4:K_ONE4 + G4]
                    ins = nc.vector.tensor_copy(Cx[s][QROWS:KROWS, b], bc(one, 2, D))
                ins.then_inc(bufs_set, 1)

            dve.wait_ge(ctx_high, 1)
            nc.vector.tensor_tensor(clow[:], craw[:], chigh[:].bitcast(F32), ALU.subtract).then_inc(ctx_low, 1)

            def normalise(i, s, k):
                step.done(nc.vector.bn_stats(stats[s][:], xt[s][:]))
                step.wait()
                nc.vector.tensor_copy(seen[s][:], stats[s][:])
                step.done(nc.vector.bn_aggr(mv[s][:], stats[s][:]))
                step.wait()
                nc.vector.tensor_scalar(veps[s][:], mv[s][:, 1:2], EPS, None, ALU.add).then_inc(var_ready, 1)

            def apply_norm(i, s, k):
                dve.wait_ge(rstd_ready, i * 6 + 2 * k + s + 1)
                nc.vector.tensor_scalar(xn[s][:], xt[s][:], mv[s][:, 0:1], rstd[s][:], ALU.subtract, ALU.mult).then_inc(xn_ready, 1)

            def rope(i, s):
                dve.wait_ge(qk_ready, i * 2 + s + 1)
                src = ps[:, 4 * s + 1, 0:320]
                nc.vector.tensor_tensor(qk[s][:].rearrange("p (h d) -> p h d", d=HD), src.rearrange("p (h d) -> p h d", d=HD),
                                        bc(K[:, K_COS1:K_COS1 + HD], 1, HEADS + KV), ALU.mult)
                q4 = src.rearrange("p (h e d) -> p h e d", e=2, d=HD // 2)
                sin = bc(K[:, K_SIN1:K_SIN1 + HD], 1, HEADS + KV).rearrange("p h (e d) -> p h e d", e=2)
                r4 = rot[s][:].rearrange("p (h e d) -> p h e d", e=2, d=HD // 2)
                step.done(nc.vector.tensor_tensor(r4, q4[:, :, ::-1, :], sin, ALU.mult))
                step.wait()
                nc.vector.tensor_tensor(qk[s][:], qk[s][:], rot[s][:], ALU.add).then_inc(rope_ready, 1)

            def place_k(i, s):
                dve.wait_ge(kT_turned, i * 2 + s + 1)
                kT = ps[0:SEQ, 4 * s + 3, 0:P].rearrange("p (b k) -> p b k", b=B2)
                nc.vector.tensor_tensor(Kbd[s][:], bc(kT, 2, BLK), bc(bc(K[0:SEQ, K_B8:K_B8 + BLK], 1, B2), 3, SEQ),
                                        ALU.mult).then_inc(k_placed, 1)

            def shift(i, s, b):
                dve.wait_ge(scored, (i * 2 + s) * B2 + b + 1)
                sc = ps[:, 4 * s + 2 * b:4 * s + 2 * b + 2, :].rearrange("p u (h k) -> p (u h) k", k=SEQ)
                m = mx[s][:, b * JP * BLK:(b + 1) * JP * BLK]
                step.done(nc.vector.tensor_reduce(m, sc, AX, ALU.max))
                step.wait()
                eb = e[s][:, b * JP:(b + 1) * JP].rearrange("p u g h k -> p (u g h) k")
                nc.vector.tensor_tensor(eb, sc, bc(m, 2, SEQ), ALU.subtract).then_inc(shifted, 1)

            def weights(i, s, b):
                dve.wait_ge(exp_ready, (i * 2 + s) * B2 + b + 1)
                u = slice(b * JP, (b + 1) * JP)
                wb = w[s][:, u].rearrange("p u g h -> p (u g h)")
                step.done(nc.vector.tensor_reduce(wb, e[s][:, u].rearrange("p u g h k -> p (u g h) k"), AX, ALU.add))
                step.wait()
                step.done(nc.vector.reciprocal(wb, wb))
                step.wait()
                nc.vector.tensor_tensor(w[s][:, u, :, 1], w[s][:, u, :, 1], lamt[:], ALU.mult).then_inc(w_ready, 1)

            def diff_sums(i, s, b):
                dve.wait_ge(relu_ready, (i * 2 + s) * B2 + b + 1)
                ds = dsum[s][:, b * JP * KV:(b + 1) * JP * KV]
                step.done(nc.vector.tensor_reduce(ds, d[s][:, b * JP:(b + 1) * JP].rearrange("p u g k -> p (u g) k"), AX, ALU.add))
                step.wait()
                step.done(nc.vector.tensor_scalar(ds, ds, 1e-6, None, ALU.add))
                step.wait()
                nc.vector.reciprocal(ds, ds).then_inc(dsum_ready, 1)

            def keep_pT(i, s):
                dve.wait_ge(pT_turned[1], i * 2 + s + 1)
                nc.vector.tensor_copy(PT[s][:, 2:4].rearrange("p u g q -> p (u g q)"), ps[:, 4 * s + 1, :]).then_inc(pT_ready[1], 1)

            def add_attention(i, s):
                dve.wait_ge(attn_ready, i * 2 + s + 1)
                step.done(nc.vector.tensor_tensor(xt[s][:], ps[:, 4 * s + 3, 0:D], xt[s][:], ALU.add))
                step.wait()

            def low_xn(i, s):
                dve.wait_ge(xn_high, i * 2 + s + 1)
                nc.vector.tensor_tensor(xnl[s][:], xn[s][:], xnh[s][:].bitcast(F32), ALU.subtract).then_inc(xn_low, 1)

            def maxima(i, s):
                for n in range(SU):
                    b, c = n // C, n % C
                    dve.wait_ge(s_ready, (i * 2 + s) * SU + n + 1)
                    sc = ps[:, 4 * s + 2 * (n % 2):4 * s + 2 * (n % 2) + 2, :].rearrange("p u (g n) -> p (u g) n", g=2)
                    nc.vector.tensor_reduce(smax[s][:, :, b, c], sc, AX, ALU.max, negate=True).then_inc(s_max, 1)

            def divide(i, s):
                dve.wait_ge(pvx_done, (i * 2 + s + 1) * GT)
                o = ps[:, 4 * s + 3, 0:C * GT * 9].rearrange("p (n d) -> p n d", d=9)
                step.done(nc.vector.reciprocal(rden[s][:], o[:, :, 8]))
                step.wait()
                nc.vector.tensor_tensor(ret[s][:].rearrange("p c (g d) -> p (c g) d", d=8), o[:, :, 0:8], bc(rden[s][:], 2, 8),
                                        ALU.mult).then_inc(ret_ready, 1)

            def add_cross(i, s):
                t = i * 2 + s
                dve.wait_ge(ret_turned, i * 2 + s + 1)
                nc.vector.tensor_tensor(X[:, t, :], ps[:, 4 * s, 0:D], xt[s][:], ALU.add)
                step.done(nc.vector.tensor_tensor(xt[s][:], ps[:, 4 * s, 0:D], xt[s][:], ALU.add))
                step.wait()

            def low_part(i, s):
                t = i * 2 + s
                dve.wait_ge(xh_ready, i * 2 + s + 1)
                nc.vector.tensor_tensor(xl[:, :, bass.ds(t * P, P)], xT[s][:], xh[:, :, bass.ds(t * P, P)].bitcast(F32),
                                        ALU.subtract).then_inc(low_ready, 1)

            with dve.Fori(0, PAIR_LOOP) as i:
                step.start(i)
                for s in range(2):
                    step.done(nc.vector.tensor_copy(xt[s][:], X[:, i * 2 + s, :]))
                    step.wait()
                    normalise(i, s, 0)
                for s in range(2):
                    apply_norm(i, s, 0)
                for s in range(2):
                    rope(i, s)
                for s in range(2):
                    place_k(i, s)
                for s in range(2):
                    for b in range(B2):
                        shift(i, s, b)
                for s in range(2):
                    for b in range(B2):
                        weights(i, s, b)
                for s in range(2):
                    for b in range(B2):
                        diff_sums(i, s, b)
                for s in range(2):
                    keep_pT(i, s)
                for s in range(2):
                    add_attention(i, s)
                    normalise(i, s, 1)
                for s in range(2):
                    apply_norm(i, s, 1)
                    low_xn(i, s)
                for s in range(2):
                    maxima(i, s)
                for s in range(2):
                    divide(i, s)
                for s in range(2):
                    add_cross(i, s)
                    normalise(i, s, 2)
                for s in range(2):
                    apply_norm(i, s, 2)
                for s in range(2):
                    low_part(i, s)
                step.end()

            dve.wait_ge(logits_kept, TILES)
            soft = Steps(dve, soft_step, 5)
            soft.start(0)
            soft.done(nc.vector.tensor_tensor(logits[:], logits[:], bc(biast[:], 1, TILES), ALU.add))
            soft.wait()
            soft.done(nc.vector.tensor_reduce(sums[:], logits[:], AX, ALU.max))
            soft.wait()
            nc.vector.tensor_tensor(logits[:], logits[:], bc(sums[:], 2, E1), ALU.subtract).then_inc(l_shifted, 1)
            dve.wait_ge(l_exp, 1)
            soft.done(nc.vector.tensor_reduce(sums[:], scores[:], AX, ALU.add))
            soft.wait()
            soft.done(nc.vector.reciprocal(sums[:], sums[:]))
            soft.wait()
            soft.done(nc.vector.tensor_tensor(scores[:], scores[:], bc(sums[:], 2, E1), ALU.mult))
            soft.wait()
            rstep = Steps(dve, rank_step, RANK_STEPS)
            rstep.start(0)
            rank_and_combine(nc, dve, rstep, scores, K[:, K_TRI1:K_TRI1 + E1 * E1], E1, TOP1,
                             cmp, eq, rank, sums, comb).then_inc(comb_ready, 1)
            dve.wait_ge(comb_turned, 1)
            for n in range(2):
                nc.vector.tensor_copy(combT[:, n * 512:(n + 1) * 512], ps[0:E1, n, :]).then_inc(combT_ready, 1)

        @block.scalar
        def _(act):
            def keep_xT(i, s, n):
                act.wait_ge(xn_turned, i * 4 + 2 * n + s + 1)
                nc.scalar.copy(xT[s][:], ps[:, 4 * s, 0:D].rearrange("p (c t) -> p c t", c=C)).then_inc(xT_ready, 1)

            def place_v(i, s):
                act.wait_ge(v_ready, i * 2 + s + 1)
                for h in range(2):
                    at = slice(h * SEQ, (h + 1) * SEQ)
                    src = ps[at, 4 * s + 2, 0:B2 * 2 * HD].rearrange("p (b g d) -> p b g d", b=B2, g=2)
                    ins = nc.scalar.copy(Vbd[s][at, :, :, h * HD:(h + 1) * HD], src)
                ins.then_inc(v_placed, 1)

            def keep_qT(i, s):
                act.wait_ge(qT_turned, i * 2 + s + 1)
                for h in range(2):
                    src = ps[h * SEQ:(h + 1) * SEQ, 4 * s, 0:D].rearrange("p (j b q) -> p b j q", j=JP, b=B2)
                    ins = nc.scalar.copy(qT[s][:, :, :, h, :], src)
                ins.then_inc(qT_ready, 1)

            def exps(i, s, b):
                act.wait_ge(shifted, (i * 2 + s) * B2 + b + 1)
                eb = e[s][:, b * JP:(b + 1) * JP].rearrange("p u g h k -> p (u g h k)")
                nc.scalar.activation(eb, eb, ACT.Exp, scale=SC).then_inc(exp_ready, 1)

            def relu(i, s, b):
                act.wait_ge(diff_ready, (i * 2 + s) * B2 + b + 1)
                db = d[s][:, b * JP:(b + 1) * JP].rearrange("p u g k -> p (u g k)")
                nc.scalar.activation(db, db, ACT.Relu).then_inc(relu_ready, 1)

            def keep_pT(i, s):
                act.wait_ge(pT_turned[0], i * 2 + s + 1)
                nc.scalar.copy(PT[s][:, 0:2].rearrange("p u g q -> p (u g q)"), ps[:, 4 * s, :]).then_inc(pT_ready[0], 1)

            def keep_aT(i, s):
                act.wait_ge(pv_ready, i * 2 + s + 1)
                nc.scalar.copy(aT[s][:], ps[:, 4 * s + 2, 0:D].rearrange("p (c t) -> p c t", c=C)).then_inc(aT_ready, 1)

            def copy_v(i, s):
                act.wait_ge(ctx_loaded[s], (i + 1) * 16)
                if not isinstance(i, int):
                    act.wait_ge(pvx_done, (i * 2 + s - 1) * GT)
                nc.scalar.copy(VT[s][:, :, :, 0:8], vraw[s][:].rearrange("p c (g d) -> p c g d", d=8)).then_inc(vt_ready, 1)

            def high_xn(i, s):
                act.wait_ge(xn_ready, i * 6 + 2 + s + 1)
                nc.scalar.copy(xnh[s][:], xn[s][:]).then_inc(xn_high, 1)

            def keep_max(i, s):
                act.wait_ge(max_turned, i * 2 + s + 1)
                nc.scalar.copy(rowmax[s][:], ps[0:G4 * SB * C, 4 * s, 0:P]).then_inc(max_high, 1)

            def x_exps(i, s):
                for g in range(GT):
                    act.wait_ge(st_ready, (i * 2 + s) * GT + g + 1)
                    if g >= RING:
                        act.wait_ge(pvx_done, (i * 2 + s) * GT + g - RING + 1)
                    nc.scalar.activation(PX[g % RING][s][:].rearrange("p c m -> p (c m)"), ps[:, 4 * s + g % 3, :], ACT.Exp,
                                         scale=XSC).then_inc(px_ready, 1)

            def high_part(i, s):
                t = i * 2 + s
                act.wait_ge(xT_ready, i * 4 + 2 + s + 1)
                nc.scalar.copy(xh[:, :, bass.ds(t * P, P)], xT[s][:]).then_inc(xh_ready, 1)

            def keep_logits(i, s):
                t = i * 2 + s
                act.wait_ge(logits_ready, i * 2 + s + 1)
                nc.scalar.copy(logits[:, t, :], ps[:, 4 * s + 1, 0:E1]).then_inc(logits_kept, 1)

            def body(i):
                for s in range(2):
                    keep_xT(i, s, 0)
                for s in range(2):
                    place_v(i, s)
                for s in range(2):
                    keep_qT(i, s)
                for s in range(2):
                    copy_v(i, s)
                for s in range(2):
                    for b in range(B2):
                        exps(i, s, b)
                for s in range(2):
                    for b in range(B2):
                        relu(i, s, b)
                for s in range(2):
                    keep_pT(i, s)
                for s in range(2):
                    keep_aT(i, s)
                for s in range(2):
                    high_xn(i, s)
                for s in range(2):
                    keep_max(i, s)
                for s in range(2):
                    x_exps(i, s)
                for s in range(2):
                    keep_xT(i, s, 1)
                    high_part(i, s)
                for s in range(2):
                    keep_logits(i, s)

            act.wait_ge(craw_loaded, 16)
            nc.scalar.copy(chigh[:], craw[:]).then_inc(ctx_high, 1)
            act.wait_ge(bufs_set, 3)
            body(0)
            with act.Fori(1, PAIR_LOOP) as i:
                body(i)
            act.wait_ge(l_shifted, 1)
            nc.scalar.activation(scores[:], logits[:], ACT.Exp).then_inc(l_exp, 1)

        @block.tensor
        def _(pe):
            def turn_xn(i, s, k, bank=0):
                pe.wait_ge(xn_ready, i * 6 + 2 * k + s + 1)
                for c in range(C):
                    mm = nc.tensor.transpose(ps[:, 4 * s + bank, c * P:(c + 1) * P], xn[s][:, c * P:(c + 1) * P], ident)
                mm.then_inc(xn_turned, 1)

            def project(i, s):
                pe.wait_ge(xT_ready, i * 4 + s + 1)
                for c in range(C):
                    mm = nc.tensor.matmul(ps[:, 4 * s + 1, 0:320], xT[s][:, c, :], W[:, c, W_QK:W_QK + 320],
                                          start=(c == 0), stop=(c == C - 1))
                mm.then_inc(qk_ready, 1)
                for b in range(B2):
                    for h in range(2):
                        rows = slice(h * SEQ, (h + 1) * SEQ)
                        for c in range(C):
                            wv = W[:, c, W_V:W_V + KV * HD].rearrange("p (n h d) -> p n h d", h=2, d=HD)[:, :, h, :]
                            dst = ps[rows, 4 * s + 2, b * 2 * HD:(b + 1) * 2 * HD].rearrange("p (n d) -> p n d", d=HD)
                            mm = nc.tensor.matmul(dst, xT[s][:, c, b * SEQ:(b + 1) * SEQ], wv, start=(c == 0), stop=(c == C - 1))
                mm.then_inc(v_ready, 1)

            def turn_qk(i, s):
                pe.wait_ge(rope_ready, i * 2 + s + 1)
                for j in range(JP):
                    mm = nc.tensor.transpose(ps[:, 4 * s, j * P:(j + 1) * P], qk[s][:, j * P:(j + 1) * P], ident)
                mm.then_inc(qT_turned, 1)
                nc.tensor.transpose(ps[0:SEQ, 4 * s + 3, 0:P], qk[s][:, D:D + SEQ], ident).then_inc(kT_turned, 1)

            def score(i, s):
                pe.wait_ge(v_placed, i * 2 + s + 1)
                pe.wait_ge(qT_ready, i * 2 + s + 1)
                pe.wait_ge(k_placed, i * 2 + s + 1)
                for b in range(B2):
                    for j in range(JP):
                        bank = ps[:, 4 * s + b * JP + j, :]
                        nc.tensor.matmul(bank.rearrange("p (h k) -> p h k", k=SEQ), idb[:], bc(causal[:], 1, BLK),
                                         start=True, stop=False)
                        mm = nc.tensor.matmul(bank, qT[s][:, b, j].rearrange("p h q -> p (h q)"),
                                              Kbd[s][:, b].rearrange("p h k -> p (h k)"), start=False, stop=True)
                    mm.then_inc(scored, 1)

            def turn_probs(i, s):
                for b in range(B2):
                    pe.wait_ge(probs_ready, (i * 2 + s) * B2 + b + 1)
                    for n in range(4):
                        part = d[s][:, b * JP + n // 2, 2 * (n % 2):2 * (n % 2) + 2].rearrange("p g k -> p (g k)")
                        mm = nc.tensor.transpose(ps[:, 4 * s + b, n * P:(n + 1) * P], part, ident)
                    mm.then_inc(pT_turned[b], 1)

            def weigh_values(i, s):
                for b in range(B2):
                    pe.wait_ge(pT_ready[b], i * 2 + s + 1)
                    for n in range(4):
                        j, g, r = n // 2, n % 2, 32 * n
                        dst = ps[r:r + 32, 4 * s + 2, 0:D].rearrange("p (h b q) -> p b h q", h=2, b=B2)[:, b]
                        mm = nc.tensor.matmul(dst, Vbd[s][:, b, g, :], PT[s][:, b * JP + j, g, :].rearrange("p (h q) -> p h q", h=2),
                                              start=True, stop=True, tile_position=(0, r))
                mm.then_inc(pv_ready, 1)

            def project_out(i, s):
                pe.wait_ge(aT_ready, i * 2 + s + 1)
                for c in range(C):
                    mm = nc.tensor.matmul(ps[:, 4 * s + 3, 0:D], aT[s][:, c, :], W[:, c, W_O:W_O + D],
                                          start=(c == 0), stop=(c == C - 1))
                mm.then_inc(attn_ready, 1)

            def x_scores(i, s):
                pe.wait_ge(ctx_placed[s], (i + 1) * 12 * 16)
                pe.wait_ge(q_placed[s], (i + 1) * 12 * 16)
                for n in range(SU):
                    b, c = n // C, n % C
                    if n >= 2:
                        pe.wait_ge(s_max, (i * 2 + s) * SU + n - 1)
                    for h in range(2):
                        mm = nc.tensor.matmul(ps[:, 4 * s + 2 * (n % 2) + h, :], Q[s][0:QROWS, b, c * P:(c + 1) * P],
                                              Cx[s][0:QROWS, b, 2 * h:2 * h + 2, :].rearrange("p g n -> p (g n)"), start=True, stop=True)
                    mm.then_inc(s_ready, 1)

            def turn_max(i, s):
                pe.wait_ge(s_max, (i * 2 + s + 1) * SU)
                nc.tensor.transpose(ps[0:G4 * SB * C, 4 * s, 0:P], smax[s][:].rearrange("p g b c -> p (g b c)"), ident).then_inc(max_turned, 1)

            def x_attend(i, s):
                pe.wait_ge(max_placed[s], (i + 1) * G4 * 16)
                pe.wait_ge(vt_ready, i * 2 + s + 1)
                for g in range(GT + 2):
                    if g < GT:
                        if g >= 3:
                            pe.wait_ge(px_ready, (i * 2 + s) * GT + g - 2)
                        for c in range(C):
                            mm = nc.tensor.matmul(ps[:, 4 * s + g % 3, c * D:(c + 1) * D], Cx[s][0:KROWS, g // G4, g % G4, c * P:(c + 1) * P],
                                                  Q[s][0:KROWS, g // G4, :], start=True, stop=True)
                        mm.then_inc(st_ready, 1)
                    if g >= 2:
                        o = g - 2
                        pe.wait_ge(px_ready, (i * 2 + s) * GT + o + 1)
                        for m in range(C):
                            at = (m * GT + o) * 9
                            for c in range(C):
                                mm = nc.tensor.matmul(ps[:, 4 * s + 3, at:at + 9], PX[o % RING][s][:, c, m * P:(m + 1) * P],
                                                      VT[s][:, c, o, :], start=(c == 0), stop=(c == C - 1))
                        mm.then_inc(pvx_done, 1)

            def turn_ret(i, s):
                pe.wait_ge(ret_ready, i * 2 + s + 1)
                for c in range(C):
                    mm = nc.tensor.transpose(ps[:, 4 * s, c * P:(c + 1) * P], ret[s][:, c, :], ident)
                mm.then_inc(ret_turned, 1)

            def route(i, s):
                pe.wait_ge(xT_ready, i * 4 + 2 + s + 1)
                for c in range(C):
                    mm = nc.tensor.matmul(ps[:, 4 * s + 1, 0:E1], xT[s][:, c, :], W[:, c, W_R:W_R + E1],
                                          start=(c == 0), stop=(c == C - 1))
                mm.then_inc(logits_ready, 1)

            pe.wait_ge(loaded, 64)
            pe.wait_ge(set_up, 2)
            with pe.Fori(0, PAIR_LOOP) as i:
                for s in range(2):
                    turn_xn(i, s, 0)
                for s in range(2):
                    project(i, s)
                for s in range(2):
                    turn_qk(i, s)
                for s in range(2):
                    score(i, s)
                for s in range(2):
                    turn_probs(i, s)
                for s in range(2):
                    weigh_values(i, s)
                for s in range(2):
                    project_out(i, s)
                for s in range(2):
                    x_scores(i, s)
                for s in range(2):
                    turn_max(i, s)
                for s in range(2):
                    x_attend(i, s)
                for s in range(2):
                    turn_ret(i, s)
                for s in range(2):
                    turn_xn(i, s, 2)
                for s in range(2):
                    route(i, s)
            pe.wait_ge(comb_ready, 1)
            for t in range(TILES):
                mm = nc.tensor.transpose(ps[0:E1, t // 4, (t % 4) * P:(t % 4 + 1) * P], comb[:, t, :], ident)
            mm.then_inc(comb_turned, 1)
    end_program(nc, semaphores)


def tables():
    k = np.zeros((P, K_ALL), np.float32)
    p = np.arange(P)
    k[:, K_ID:K_ID + P] = np.eye(P)
    freq = (10000.0 ** (-np.arange(0, HD, 2) / HD)).astype(np.float32)
    angle = ((p % SEQ).astype(np.float32)[:, None] * freq[None]).astype(np.float64)
    cos, sin = np.cos(angle), np.sin(angle)
    k[:, K_COS:K_COS + HD] = np.repeat(cos, 2, axis=1)
    k[:, K_COS1:K_COS1 + HD] = np.concatenate([cos, cos], axis=1)
    k[:, K_SIN0:K_SIN0 + HD] = np.stack([-sin, sin], axis=-1).reshape(P, HD)
    k[:, K_SIN1:K_SIN1 + HD] = np.concatenate([-sin, sin], axis=1)
    k[:, K_H16:K_H16 + CH] = p[:, None] // HD == np.arange(CH)
    k[:, K_B8:K_B8 + 8] = p[:, None] // 8 == np.arange(8)
    k[:, K_CAUSAL:K_CAUSAL + SEQ] = np.where(np.arange(SEQ)[None] <= p[:, None] % SEQ, 0.0, NEG)
    for at, n in ((K_TRI0, E0), (K_TRI1, E1)):
        k[:, at:at + n * n] = (np.arange(n)[None] < np.arange(n)[:, None]).reshape(-1)
    k[:, K_ONE4:K_ONE4 + G4] = p[:, None] % 32 == np.arange(G4)
    return k


def kernel(x, ctx_2048, mask_BxS2_bk0, L0_attn_Wq, L0_attn_Wk, L0_attn_Wv, L0_attn_Wo, L0_ffn_w_router, L0_ffn_wg,
           L0_ffn_wu, L0_ffn_wd, L0_ffn_sg, L0_ffn_su, L0_ffn_sd, L1_attn_Wq, L1_attn_Wk, L1_attn_Wv, L1_attn_Wo,
           L1_attn_lam, L1_ffn_router_w, L1_ffn_expert_bias, L1_ffn_gate_proj, L1_ffn_up_proj, L1_ffn_down_proj):
    import concourse.bacc as _bacc
    from concourse.bass_utils import run_bass_kernel_spmd as _run

    a = {n: np.asarray(v) for n, v in locals().items() if not n.startswith("_")}

    def rows(w):
        return w.reshape(C, P, -1).transpose(1, 0, 2)

    def chunks(gate, up, down, n):
        g = gate.reshape(C, P, n, P).transpose(2, 1, 0, 3).reshape(n, P, D)
        u = up.reshape(C, P, n, P).transpose(2, 1, 0, 3).reshape(n, P, D)
        return np.concatenate([g, u, down.reshape(n, P, D)], axis=2)

    ctx = a["ctx_2048"]
    wq1 = a["L1_attn_Wq"].reshape(D, KV, 2 * JP, HD).transpose(0, 2, 1, 3).reshape(D, D)
    wo1 = a["L1_attn_Wo"].reshape(2, 2, JP, 2, HD, D).transpose(3, 2, 0, 1, 4, 5).reshape(D, D)
    w_attn0 = np.concatenate([a["L0_attn_Wq"].T, a["L0_attn_Wk"].T, a["L0_attn_Wv"].T, a["L0_attn_Wo"].T,
                              a["L0_ffn_w_router"].T], axis=1)
    w_attn1 = np.concatenate([wq1, a["L1_attn_Wk"], a["L1_attn_Wv"], wo1, a["L1_ffn_router_w"].T], axis=1)
    gate0, up0, down0 = (np.concatenate([a["L0_ffn_w" + n], a["L0_ffn_s" + n]]) for n in "gud")
    arrays = {
        "x": a["x"].reshape(TILES, P, D).transpose(1, 0, 2),
        "consts": tables(),
        "w_attn0": rows(w_attn0),
        "ctx_rows": ctx.reshape(TILES, P, D),
        "ctx_cols": ctx.reshape(TILES, P, C, P).transpose(0, 3, 2, 1),
        "ctx_lhs": ctx.reshape(TILES, GT, 8, C, P).transpose(0, 4, 3, 1, 2),
        "mask": a["mask_BxS2_bk0"].view(np.int32).reshape(TILES, B2, SEQ // 4).transpose(1, 0, 2),
        "w_ffn0": chunks(gate0.reshape(-1, D).T, up0.reshape(-1, D).T, down0.transpose(0, 2, 1).reshape(-1, D), CHUNKS0),
        "w_attn1": rows(w_attn1),
        "lam": a["L1_attn_lam"].reshape(KV, JP, 2).transpose(2, 1, 0),
        "bias1": a["L1_ffn_expert_bias"],
        "w_ffn1": chunks(a["L1_ffn_gate_proj"].transpose(1, 0, 2).reshape(D, -1),
                         a["L1_ffn_up_proj"].transpose(1, 0, 2).reshape(D, -1),
                         a["L1_ffn_down_proj"].reshape(-1, D), CHUNKS1),
    }
    nc = _bacc.Bacc("TRN2", target_bir_lowering=False, num_devices=1)
    arrays = {n: np.ascontiguousarray(v) for n, v in arrays.items()}
    args = [nc.dram_tensor(n, v.shape, mybir.dt.from_np(v.dtype), kind="ExternalInput").ap() for n, v in arrays.items()]
    out = nc.dram_tensor("out", (P, TILES, D), F32, kind="ExternalOutput").ap()
    ctx_parts = nc.dram_tensor("ctx_parts", (2, TILES, P, D), F32).ap()
    comb0 = nc.dram_tensor("comb0", (E0 + SHARED0, TOKENS), F32).ap()
    comb1 = nc.dram_tensor("comb1", (E1, TOKENS), F32).ap()
    decoder_kernel(nc, *args, out, ctx_parts, comb0, comb1)
    r = _run(nc, [arrays], core_ids=[0])
    return r.results[0]["out"].transpose(1, 0, 2).reshape(BATCH, SEQ, D)
```
